# Optimizing a Trainium2 kernel written in Bass

```python
import numpy as np
import jax
import jax.numpy as jnp

def _softmax(x, axis=-1):
    return jax.nn.softmax(x, axis=axis)

def _gelu(x):
    return jax.nn.gelu(x, approximate=True)

def _silu(x):
    return jax.nn.silu(x)

def _sigmoid(x):
    return jax.nn.sigmoid(x)

def _layernorm(x, axis=-1, eps=1e-05):
    m = jnp.mean(x, axis=axis, keepdims=True)
    v = jnp.var(x, axis=axis, keepdims=True)
    return (x - m) / jnp.sqrt(v + eps)

def _scatter_add(tgt, idx, src, axis=0):
    return tgt.at[idx].add(src)

def _segment_sum(src, seg, n):
    return jax.ops.segment_sum(src, seg, n)
kernel_name = 'mk_hybrid_d1_jaxref_r8_d919fb'

def setup_inputs(seed: int=0):
    np.random.seed(seed)
    _w = jnp.asarray

    def _L0_attn_a_setup():
        import jax, jax.numpy as jnp
        import numpy as np
        DIM = 128
        B, S = (8, 256)
        LN_EPS = 1e-05
        key = jax.random.key(seed)
        k1, k2, k3 = jax.random.split(key, 3)
        x = jax.random.normal(k1, (B, S, DIM), dtype=jnp.float32)
        w_qkv = jax.random.normal(k2, (3 * DIM, DIM), dtype=jnp.float32) * np.sqrt(2.0 / (DIM + 3 * DIM))
        w_fc = jax.random.normal(k3, (DIM, DIM), dtype=jnp.float32) * np.sqrt(2.0 / (DIM + DIM))
        b_fc = jnp.zeros((DIM,), dtype=jnp.float32)
        gamma = jnp.ones((DIM,), dtype=jnp.float32)
        beta = jnp.zeros((DIM,), dtype=jnp.float32)
        return {'x': x, 'w_qkv': w_qkv, 'w_fc': w_fc, 'b_fc': b_fc, 'gamma': gamma, 'beta': beta}
    _L0_attn_a_in = _L0_attn_a_setup()

    def _L0_attn_b_setup():
        import jax, jax.numpy as jnp
        import numpy as np
        B, T, HID = (16, 64, 128)
        NH, NKV, D = (8, 4, 128)
        THETA = 10000.0

        def _rotate_half(x):
            x1, x2 = (x[..., :x.shape[-1] // 2], x[..., x.shape[-1] // 2:])
            return jnp.concatenate((-x2, x1), axis=-1)
        key = jax.random.key(seed)
        k0, k1, k2, k3, k4 = jax.random.split(key, 5)
        s = 0.02
        return {'hidden_states': jax.random.normal(k0, (B, T, HID), dtype=jnp.float32), 'Wq': s * jax.random.normal(k1, (HID, NH * D), dtype=jnp.float32), 'Wk': s * jax.random.normal(k2, (HID, NKV * D), dtype=jnp.float32), 'Wv': s * jax.random.normal(k3, (HID, NKV * D), dtype=jnp.float32), 'Wo': s * jax.random.normal(k4, (NH * D, HID), dtype=jnp.float32)}
    _L0_attn_b_in = _L0_attn_b_setup()

    def _L0_ffn_setup():
        import jax, jax.numpy as jnp
        import numpy as np
        N, T, D = (4, 512, 128)
        NUM_EXPERTS = 8
        EXPERT_CAP = 2.0
        MLP_RATIO = 4
        HIDDEN = MLP_RATIO * D
        key = jax.random.key(seed)
        k1, k2, k3, k4 = jax.random.split(key, 4)
        x = jax.random.normal(k1, (N, T, D), dtype=jnp.float32)
        gate_w = jax.random.truncated_normal(k2, -2.0, 2.0, (D, NUM_EXPERTS), dtype=jnp.float32) * 0.02
        w1 = jax.random.normal(k3, (NUM_EXPERTS, D, HIDDEN), dtype=jnp.float32) * 0.02
        w2 = jax.random.normal(k4, (NUM_EXPERTS, HIDDEN, D), dtype=jnp.float32) * 0.02
        return {'x': x, 'gate_w': gate_w, 'w1': w1, 'w2': w2}
    _L0_ffn_in = _L0_ffn_setup()
    _d = {'L0_attn_a_x': _L0_attn_a_in['x'], 'L0_attn_a_w_qkv': _L0_attn_a_in['w_qkv'], 'L0_attn_a_w_fc': _L0_attn_a_in['w_fc'], 'L0_attn_a_b_fc': _L0_attn_a_in['b_fc'], 'L0_attn_a_gamma': _L0_attn_a_in['gamma'], 'L0_attn_a_beta': _L0_attn_a_in['beta'], 'L0_attn_b_Wq': _L0_attn_b_in['Wq'], 'L0_attn_b_Wk': _L0_attn_b_in['Wk'], 'L0_attn_b_Wv': _L0_attn_b_in['Wv'], 'L0_attn_b_Wo': _L0_attn_b_in['Wo'], 'L0_ffn_gate_w': _L0_ffn_in['gate_w'], 'L0_ffn_w1': _L0_ffn_in['w1'], 'L0_ffn_w2': _L0_ffn_in['w2']}
    _x0 = _d['L0_attn_a_x']
    _d['L0_attn_a_x'] = jax.random.normal(jax.random.fold_in(jax.random.key(seed), 1), (4, 1024, 128), dtype=_x0.dtype)
    del _x0
    return _d

def reference(L0_attn_a_x, L0_attn_a_w_qkv, L0_attn_a_w_fc, L0_attn_a_b_fc, L0_attn_a_gamma, L0_attn_a_beta, L0_attn_b_Wq, L0_attn_b_Wk, L0_attn_b_Wv, L0_attn_b_Wo, L0_ffn_gate_w, L0_ffn_w1, L0_ffn_w2):

    def _L0_attn_a_ref(x, w_qkv, w_fc, b_fc, gamma, beta):
        import jax, jax.numpy as jnp
        import numpy as np
        DIM = 128
        B, S = (8, 256)
        LN_EPS = 1e-05
        scaling = DIM ** (-0.5)
        qkv = jnp.einsum('bsd,ed->bse', x, w_qkv)
        q, k, v = jnp.split(qkv, 3, axis=-1)
        att = jax.nn.softmax(jnp.einsum('bqd,bkd->bqk', q, k) * scaling, axis=-1)
        y = jnp.einsum('bqk,bvd->bqd', att, v)
        y = jnp.einsum('bqd,ed->bqe', y, w_fc) + b_fc
        h = x + y
        mu = jnp.mean(h, axis=-1, keepdims=True)
        var = jnp.var(h, axis=-1, keepdims=True)
        return (h - mu) * jax.lax.rsqrt(var + LN_EPS) * gamma + beta

    def _L0_attn_b_ref(hidden_states, Wq, Wk, Wv, Wo):
        import jax, jax.numpy as jnp
        import numpy as np
        B, T, HID = (16, 64, 128)
        NH, NKV, D = (8, 4, 128)
        THETA = 10000.0

        def _rotate_half(x):
            x1, x2 = (x[..., :x.shape[-1] // 2], x[..., x.shape[-1] // 2:])
            return jnp.concatenate((-x2, x1), axis=-1)
        b, t, _ = hidden_states.shape
        q = (hidden_states @ Wq).reshape(b, t, NH, D).transpose(0, 2, 1, 3)
        k = (hidden_states @ Wk).reshape(b, t, NKV, D).transpose(0, 2, 1, 3)
        v = (hidden_states @ Wv).reshape(b, t, NKV, D).transpose(0, 2, 1, 3)
        inv_freq = 1.0 / THETA ** (jnp.arange(0, D, 2, dtype=jnp.float32) / D)
        freqs = jnp.outer(jnp.arange(t, dtype=jnp.float32), inv_freq)
        emb = jnp.concatenate((freqs, freqs), axis=-1)
        cos, sin = (jnp.cos(emb), jnp.sin(emb))
        q = q * cos + _rotate_half(q) * sin
        k = k * cos + _rotate_half(k) * sin
        groups = NH // NKV
        k = jnp.repeat(k, groups, axis=1)
        v = jnp.repeat(v, groups, axis=1)
        scale = 1.0 / jnp.sqrt(jnp.float32(D))
        attn = jnp.einsum('bhtd,bhsd->bhts', q, k) * scale
        causal = jnp.triu(jnp.ones((t, t), dtype=bool), k=1)
        attn = jnp.where(causal, -jnp.inf, attn)
        attn = jax.nn.softmax(attn, axis=-1)
        out = jnp.einsum('bhts,bhsd->bhtd', attn, v)
        out = out.transpose(0, 2, 1, 3).reshape(b, t, NH * D)
        return out @ Wo

    def _L0_ffn_ref(x, gate_w, w1, w2):
        import jax, jax.numpy as jnp
        import numpy as np
        N, T, D = (4, 512, 128)
        NUM_EXPERTS = 8
        EXPERT_CAP = 2.0
        MLP_RATIO = 4
        HIDDEN = MLP_RATIO * D
        x = x.astype(jnp.float32)
        n, t, d = x.shape
        k = int(EXPERT_CAP * t / NUM_EXPERTS)
        scores = jnp.einsum('ntd,de->nte', x, gate_w)
        probs = jax.nn.softmax(scores, axis=-1)
        probs = jnp.transpose(probs, (0, 2, 1))
        g, m = jax.lax.top_k(probs, k)
        xin = jax.vmap(lambda xb, mb: xb[mb])(x, m)
        h = jax.nn.gelu(jnp.einsum('nekd,edf->nekf', xin, w1))
        h = jnp.einsum('nekf,efd->nekd', h, w2)
        weighted = g[..., None] * h
        flat_idx = (m + jnp.arange(n, dtype=m.dtype)[:, None, None] * t).reshape(-1)
        out = jnp.zeros((n * t, d), dtype=jnp.float32).at[flat_idx].add(weighted.reshape(-1, d))
        out = out.reshape(n, t, d)
        return out.astype(jnp.bfloat16)
    x = L0_attn_a_x
    x = x + _L0_attn_a_ref(_layernorm(x, axis=-1), L0_attn_a_w_qkv, L0_attn_a_w_fc, L0_attn_a_b_fc, L0_attn_a_gamma, L0_attn_a_beta)
    x = x + _L0_ffn_ref(_layernorm(x, axis=-1), L0_ffn_gate_w, L0_ffn_w1, L0_ffn_w2)
    x = x + _L0_attn_b_ref(_layernorm(x, axis=-1), L0_attn_b_Wq, L0_attn_b_Wk, L0_attn_b_Wv, L0_attn_b_Wo)
    x = x + _L0_ffn_ref(_layernorm(x, axis=-1), L0_ffn_gate_w, L0_ffn_w1, L0_ffn_w2)
    return x

_drawn_inputs = setup_inputs


def setup_inputs(seed=0):
    import zlib

    import numpy as np

    out = dict(_drawn_inputs(seed))
    spreads = {'L0_attn_a_b_fc': (0.0, 2.0), 'L0_attn_a_gamma': (1.0, 0.2), 'L0_attn_a_beta': (0.0, 0.1)}
    factors = {'L0_attn_b_Wq': 8.0,
     'L0_attn_b_Wk': 8.0,
     'L0_ffn_gate_w': 4.251,
     'L0_ffn_w1': 3.795,
     'L0_ffn_w2': 3.714}
    for name, (base, spread) in spreads.items():
        noise = np.random.default_rng([zlib.crc32(name.encode()), seed]).standard_normal(out[name].shape)
        drawn = base * np.exp(spread * noise) if base else spread * noise
        out[name] = jnp.asarray(drawn.astype(out[name].dtype))
    for name, factor in factors.items():
        out[name] = (out[name] * factor).astype(out[name].dtype)
    return out
```

```python
import concourse.bass as bass
from concourse import mybir
from contextlib import ExitStack

F32 = mybir.dt.float32
F16 = mybir.dt.float16
BF16 = mybir.dt.bfloat16
U32 = mybir.dt.uint32
ALU = mybir.AluOpType
ACT = mybir.ActivationFunctionType
AX_X = mybir.AxisListType.X

P = 128
B, S = 4, 1024
T = S // P
NT = B * T
NH, NKV = 8, 4
GROUP = NH // NKV
E = 8
FC = 4
CAP = 2 * S // E
CH = CAP // P
ROWS = E * B
SCALE = float(P) ** -0.5
EPS = 1e-5
STAGES = 4
ONE = 1
WS = 64.0


class Steps:

    def __init__(self, sem):
        self.sem, self.base, self.n, self.outer = sem, ONE, 0, []

    @property
    def at(self):
        return self.base + self.n

    def step(self, instruction, n=1):
        instruction.then_inc(self.sem, n)
        self.n += n
        return self.at

    def expect(self, n=1):
        self.n += n
        return self.at

    def enter(self, i, per):
        self.outer.append((self.base, self.n, per))
        self.base, self.n = self.base + self.n + i * per, 0

    def leave(self, rounds):
        base, n, per = self.outer.pop()
        assert self.n == per, (self.sem, self.n)
        self.base, self.n = base, n + rounds * per


def flat(ap):
    return ap.rearrange("p a b -> p (a b)")


class Net:

    def __init__(self, nc, ctx):
        self.nc, self.ctx = nc, ctx
        self.n = 0

    def sb(self, ctx, name, shape, dt=F32):
        self.n += 1
        return ctx.enter_context(self.nc.sbuf_tensor(f"{name}_{self.n}", shape, dt))

    def ps(self, ctx, name, shape, dt=F32):
        self.n += 1
        return ctx.enter_context(self.nc.psum_tensor(f"{name}_{self.n}", shape, dt))

    def sem(self, ctx, name):
        self.n += 1
        return ctx.enter_context(self.nc.semaphore(f"{name}_{self.n}"))

    def makers(self, ctx):
        self.stage_sems = []

        def sem(name, swdge=False):
            if swdge:
                return self.sem(ctx, name)
            self.stage_sems.append(self.sem(ctx, name))
            return self.stage_sems[-1]

        return (lambda *a: self.sb(ctx, *a)), (lambda *a: self.ps(ctx, *a)), sem

    def raise_sems(self):
        with self.nc.Block() as block:
            @block.sync
            def _(sp):
                for s in self.stage_sems:
                    sp.sem_inc(s, ONE)


def load_stage(net, d):
    nc, ctx = net.nc, net.ctx
    net.x = net.sb(ctx, "x", [P, NT, P])
    plain = {"wq_a": P, "wk_a": P, "wv_aT": P, "wfc_T": P, "bfc": P, "gamma": P, "beta": P, "gate": E,
             "wo": NH * P, "w2": E * FC * P, "cos": S, "sin": S, "ident": P, "identb": P, "maskb": P}
    net.w = {k: net.sb(ctx, k, [P, n], BF16 if k.endswith("b") and k != "gab" else F32) for k, n in plain.items()}
    net.rowbase = net.sb(ctx, "rowbase", [ROWS, 1])
    parts = {"w1": E * FC * P, "wq": NH * P, "wk": NKV * P, "wv": NKV * P}
    net.hi = {k: net.sb(ctx, k + "_hi", [P, n], F16) for k, n in parts.items()}
    net.lo = {k: net.sb(ctx, k + "_lo", [P, n], F16) for k, n in parts.items()}
    with ExitStack() as tmp:
        raw = {k: net.sb(tmp, k + "_raw", [P, n]) for k, n in parts.items()}
        s_raw = {k: net.sem(tmp, k + "_loaded") for k in parts}
        s_hi = net.sem(tmp, "hi_ready")
        s_rest = net.sem(tmp, "rest_loaded")
        with nc.Block() as block:
            @block.sync
            def _(sp):
                for k in parts:
                    sp.dma_start(raw[k][:], d[k]).then_inc(s_raw[k], 16)
                x_tiles = d["x"].rearrange("(t p) c -> p t c", p=P)
                n = 0
                for b in range(B):
                    sp.dma_start(net.x[:, b * T:(b + 1) * T, :], x_tiles[:, b * T:(b + 1) * T, :]).then_inc(s_rest, 16)
                    n += 16
                for k in plain:
                    sp.dma_start(net.w[k][:], d[k]).then_inc(s_rest, 16)
                    n += 16
                sp.dma_start(net.rowbase[:], d["rowbase"]).then_inc(s_rest, 16)
                sp.wait_ge(s_rest, n + 16)

            @block.scalar
            def _(act):
                for k in parts:
                    act.wait_ge(s_raw[k], 16)
                    nc.scalar.activation(net.hi[k][:], raw[k][:], ACT.Copy, scale=WS).then_inc(s_hi, 1)

            @block.vector
            def _(dve):
                for i, k in enumerate(parts):
                    dve.wait_ge(s_raw[k], 16)
                    dve.wait_ge(s_hi, i + 1)
                    nc.vector.scalar_tensor_tensor(net.lo[k][:], raw[k][:], WS, net.hi[k][:], ALU.mult, ALU.subtract)


def norm_stats(nc, dve, done, sem_var, sem_std, stats, work, mean, rstd, src, n, loop):
    loop(n, lambda i, k: nc.vector.bn_stats(stats[:, bass.ds(i, 1), :].rearrange("p a b -> p (a b)"), src(i)))
    dve.wait_ge(done.sem, done.at)
    me, mo, ve, vo = stats[:, :, 1], stats[:, :, 4], stats[:, :, 2], stats[:, :, 5]
    total, diff, var, sq = work[:, 0, :], work[:, 1, :], work[:, 2, :], work[:, 3, :]
    done.step(nc.vector.tensor_tensor(total, me, mo, ALU.add))
    done.step(nc.vector.tensor_tensor(diff, me, mo, ALU.subtract))
    done.step(nc.vector.tensor_tensor(var, ve, vo, ALU.add))
    dve.wait_ge(done.sem, done.at)
    done.step(nc.vector.tensor_scalar(mean, total, 0.5, None, op0=ALU.mult))
    done.step(nc.vector.tensor_tensor(sq, diff, diff, ALU.mult))
    dve.wait_ge(done.sem, done.at)
    done.step(nc.vector.tensor_scalar(sq, sq, 0.25, EPS, op0=ALU.mult, op1=ALU.add))
    dve.wait_ge(done.sem, done.at)
    sem_var.step(nc.vector.scalar_tensor_tensor(var, var, 1.0 / P, sq, ALU.mult, ALU.add))
    dve.wait_ge(sem_std.sem, sem_std.expect())
    done.step(nc.vector.reciprocal(rstd, var))
    dve.wait_ge(done.sem, done.at)


def stats_of_x(net, dve, done, s_var, s_std, stats, work, mean, rstd):
    nc = net.nc

    def loop(n, body):
        with dve.Fori(0, B) as b:
            for t in range(T):
                body(b * T + t, t).then_inc(done.sem, 1)
        done.expect(n)

    norm_stats(nc, dve, done, s_var, s_std, stats, work, mean, rstd,
               lambda i: net.x[:, bass.ds(i, 1), :].rearrange("p a b -> p (a b)"), NT, loop)


def attention_a(net):
    nc, w = net.nc, net.w
    with ExitStack() as ctx:
        sb, ps, sem = net.makers(ctx)
        stats = sb("stats", [P, NT, 6])
        work = sb("work", [P, 4, NT])
        mean, rstd = sb("mean", [P, NT]), sb("rstd", [P, NT])
        xs = sb("xs", [P, T, P])
        xT_hi, xT_lo = sb("xT_hi", [P, S], F16), sb("xT_lo", [P, S], F16)
        g_hi, g_lo = sb("g_hi", [P, P], F16), sb("g_lo", [P, P], F16)
        qg_hi, qg_lo = sb("qg_hi", [P, S], F16), sb("qg_lo", [P, S], F16)
        xsum, vsum, vsum_b, crow = sb("xsum", [P, 1]), sb("vsum", [P, 1]), sb("vsum_b", [P, P]), sb("crow", [P, P])
        prob = sb("prob", [P, 2, S])
        nmax, nbias = sb("nmax", [P, T]), sb("nbias", [P, T])
        rowsum, rinv, wsum = sb("rowsum", [P, T]), sb("rinv", [P, T]), sb("wsum", [P, T])
        h = sb("h", [P, T, P])
        hn = sb("hn", [P, T, P])
        hstats, hwork = sb("hstats", [P, T, 6]), sb("hwork", [P, 4, T])
        hmean, hrstd = sb("hmean", [P, T]), sb("hrstd", [P, T])
        psT = ps("psT", [P, S])
        psS = [ps(f"psS{i}", [P, S]) for i in range(2)]
        psC = ps("psC", [P, 512])

        s_var, s_std = sem("var"), sem("std")
        s_dve, s_pool = sem("dve"), sem("pool")
        s_g, s_ghi = sem("g"), sem("g_hi")
        s_xs, s_xT, s_xhi, s_xlo = sem("xs"), sem("xT"), sem("x_hi"), sem("x_lo")
        s_qg, s_qghi, s_qglo = sem("qg"), sem("qg_hi"), sem("qg_lo")
        s_xsum, s_v, s_vb, s_c = sem("xsum"), sem("v"), sem("v_b"), sem("c")
        s_s, s_nb, s_exp, s_hn, s_hvar, s_hstd = sem("scores"), sem("nbias"), sem("exp"), sem("hn"), sem("hvar"), sem("hstd")

        net.raise_sems()
        with nc.Block() as block:
            @block.tensor
            def _(pe):
                pe.matmul(psC[:, 0:P], w["wq_a"][:], w["wk_a"][:], start=True, stop=True).then_inc(s_g, 1)
                with pe.Fori(0, B) as b:
                    pe.wait_ge(s_xs, ONE + (b + 1) * T)
                    pe.wait_ge(s_qghi, ONE + b)
                    pe.wait_ge(s_qglo, ONE + b)
                    for t in range(T):
                        last = pe.transpose(psT[:, t * P:(t + 1) * P], xs[:, t, :], w["ident"][:])
                    last.then_inc(s_xT, 1)
                    pe.wait_ge(s_xsum, ONE + b + 1)
                    pe.matmul(psC[:, P:P + 1], w["wv_aT"][:], xsum[:], start=True, stop=True).then_inc(s_v, 1)
                    pe.wait_ge(s_vb, ONE + b + 1)
                    pe.matmul(psC[:, 2 * P:3 * P], vsum_b[:], w["wfc_T"][:], start=True, stop=True).then_inc(s_c, 1)
                    pe.wait_ge(s_xhi, ONE + b + 1)
                    pe.wait_ge(s_xlo, ONE + b + 1)
                    for c in range(2):
                        cols = slice(c * 512, (c + 1) * 512)
                        for i, (l, r) in enumerate(((g_hi, xT_hi), (g_hi, xT_lo), (g_lo, xT_hi))):
                            last = pe.matmul(psT[:, cols], l[:], r[:, cols], start=(i == 0), stop=(i == 2))
                    last.then_inc(s_qg, 1)
                    pe.wait_ge(s_qghi, ONE + b + 1)
                    pe.wait_ge(s_qglo, ONE + b + 1)
                    for t in range(T):
                        pe.wait_ge(s_exp, ONE + b * T + t - 1) if t >= 1 else pe.wait_ge(s_exp, ONE + b * T)
                        rows = slice(t * P, (t + 1) * P)
                        for c in range(2):
                            cols = slice(c * 512, (c + 1) * 512)
                            for i, (l, r) in enumerate(((qg_hi, xT_hi), (qg_hi, xT_lo), (qg_lo, xT_hi))):
                                last = pe.matmul(psS[t % 2][:, cols], l[:, rows], r[:, cols],
                                                 start=(i == 0), stop=(i == 2))
                        last.then_inc(s_s, 1)

            @block.vector
            def _(dve):
                done, var, std = Steps(s_dve), Steps(s_var), Steps(s_std)
                dve.wait_ge(s_g, ONE + 1)
                dve.wait_ge(s_ghi, ONE + 1)
                done.step(nc.vector.scalar_tensor_tensor(g_lo[:], psC[:, 0:P], WS, g_hi[:], ALU.mult, ALU.subtract))
                stats_of_x(net, dve, done, var, std, stats, work, mean[:], rstd[:])
                hvar, hstd = Steps(s_hvar), Steps(s_hstd)
                with dve.Fori(0, B) as b:
                    done.enter(b, 36)
                    hvar.enter(b, 1)
                    hstd.enter(b, 1)
                    dve.wait_ge(s_xT, ONE + b)
                    for t in range(T):
                        i = b * T + t
                        nc.vector.tensor_scalar(xs[:, t, :], net.x[:, bass.ds(i, 1), :].rearrange("p a b -> p (a b)"),
                                                mean[:, bass.ds(i, 1)], rstd[:, bass.ds(i, 1)],
                                                op0=ALU.subtract, op1=ALU.mult).then_inc(s_xs, 1)
                    dve.wait_ge(s_xT, ONE + b + 1)
                    nc.vector.reduce_sum(xsum[:], psT[:], AX_X).then_inc(s_xsum, 1)
                    dve.wait_ge(s_xhi, ONE + b + 1)
                    dve.wait_ge(s_s, ONE + b * T)
                    nc.vector.tensor_tensor(xT_lo[:], psT[:], xT_hi[:], ALU.subtract).then_inc(s_xlo, 1)
                    dve.wait_ge(s_v, ONE + b + 1)
                    done.step(nc.vector.tensor_copy(vsum[:], psC[:, P:P + 1]))
                    dve.wait_ge(done.sem, done.at)
                    nc.vector.tensor_copy(vsum_b[:], vsum[:].to_broadcast([P, P])).then_inc(s_vb, 1)
                    dve.wait_ge(s_c, ONE + b + 1)
                    done.step(nc.vector.tensor_copy(crow[:], psC[:, 2 * P:3 * P]))
                    dve.wait_ge(s_qg, ONE + b + 1)
                    dve.wait_ge(s_qghi, ONE + b + 1)
                    nc.vector.tensor_tensor(qg_lo[:], psT[:], qg_hi[:], ALU.subtract).then_inc(s_qglo, 1)
                    for t in range(T):
                        dve.wait_ge(s_s, ONE + b * T + t + 1)
                        done.step(nc.vector.reduce_max(nmax[:, t:t + 1], psS[t % 2][:], AX_X, negate=True))
                        dve.wait_ge(done.sem, done.at)
                        nc.vector.tensor_scalar(nbias[:, t:t + 1], nmax[:, t:t + 1], SCALE / WS, None,
                                                op0=ALU.mult).then_inc(s_nb, 1)
                    dve.wait_ge(s_exp, ONE + (b + 1) * T)
                    done.step(nc.vector.reciprocal(rinv[:], rowsum[:]))
                    dve.wait_ge(done.sem, done.at)
                    done.step(nc.vector.tensor_tensor(wsum[:], rinv[:], rowsum[:], ALU.mult))
                    dve.wait_ge(done.sem, done.at)
                    for t in range(T):
                        done.step(nc.vector.scalar_tensor_tensor(h[:, t, :], crow[:], wsum[:, t:t + 1], xs[:, t, :],
                                                                 ALU.mult, ALU.add))
                    dve.wait_ge(done.sem, done.at)
                    done.step(nc.vector.tensor_tensor(h[:], h[:], w["bfc"][:, None, :].to_broadcast([P, T, P]), ALU.add))
                    dve.wait_ge(done.sem, done.at)
                    def loop(n, body):
                        for t in range(n):
                            done.step(body(t, t))

                    norm_stats(nc, dve, done, hvar, hstd, hstats, hwork, hmean[:], hrstd[:],
                               lambda t: h[:, t, :], T, loop)
                    dve.wait_ge(s_pool, ONE + 3 * b)
                    for t in range(T):
                        nc.vector.tensor_scalar(hn[:, t, :], h[:, t, :], hmean[:, t:t + 1], hrstd[:, t:t + 1],
                                                op0=ALU.subtract, op1=ALU.mult).then_inc(s_hn, 1)
                    for steps in (done, hvar, hstd):
                        steps.leave(B)

            @block.scalar
            def _(act):
                act.wait_ge(s_g, ONE + 1)
                nc.scalar.activation(g_hi[:], psC[:, 0:P], ACT.Copy, scale=WS).then_inc(s_ghi, 1)
                act.wait_ge(s_var, ONE + 1)
                nc.scalar.activation(work[:, 2, :], work[:, 2, :], ACT.Sqrt).then_inc(s_std, 1)
                with act.Fori(0, B) as b:
                    act.wait_ge(s_xsum, ONE + b + 1)
                    act.wait_ge(s_s, ONE + b * T)
                    nc.scalar.activation(xT_hi[:], psT[:], ACT.Copy).then_inc(s_xhi, 1)
                    act.wait_ge(s_qg, ONE + b + 1)
                    nc.scalar.activation(qg_hi[:], psT[:], ACT.Copy).then_inc(s_qghi, 1)
                    for t in range(T):
                        act.wait_ge(s_nb, ONE + b * T + t + 1)
                        if t >= 2:
                            act.wait_ge(s_exp, ONE + b * T + t - 1)
                        else:
                            act.wait_ge(s_exp, ONE + b * T)
                        nc.scalar.activation(prob[:, t % 2, :], psS[t % 2][:], ACT.Exp, bias=nbias[:, t:t + 1],
                                             scale=SCALE / WS, accum_out=rowsum[:, t:t + 1]).then_inc(s_exp, 1)
                    act.wait_ge(s_hvar, ONE + b + 1)
                    nc.scalar.activation(hwork[:, 2, :], hwork[:, 2, :], ACT.Sqrt).then_inc(s_hstd, 1)

            @block.gpsimd
            def _(pool):
                with pool.Fori(0, B) as b:
                    rows = net.x[:, bass.ds(b * T, T), :]
                    pool.wait_ge(s_hn, ONE + (b + 1) * T)
                    nc.gpsimd.tensor_tensor(hn[:], hn[:], w["gamma"][:, None, :].to_broadcast([P, T, P]), ALU.mult).then_inc(s_pool, 1)
                    pool.wait_ge(s_pool, ONE + b * 3 + 1)
                    nc.gpsimd.tensor_tensor(hn[:], hn[:], w["beta"][:, None, :].to_broadcast([P, T, P]), ALU.add).then_inc(s_pool, 1)
                    pool.wait_ge(s_pool, ONE + b * 3 + 2)
                    nc.gpsimd.tensor_tensor(rows, rows, hn[:], ALU.add).then_inc(s_pool, 1)


def ffn(net, out_name, acc_dram, xn_dram):
    nc, w = net.nc, net.w
    with ExitStack() as outer:
        idx = net.sb(outer, "idx", [P, CH, ROWS], U32)
        weight = net.sb(outer, "weight", [P, CH, ROWS])
        ffn_route(net, acc_dram, xn_dram, idx, weight)
        ffn_experts(net, acc_dram, xn_dram, idx, weight)


def ffn_route(net, acc_dram, xn_dram, idx, weight):
    nc, w = net.nc, net.w
    ROUNDS = CAP // 8
    with ExitStack() as ctx:
        sb, ps, sem = net.makers(ctx)
        stats, work = sb("stats", [P, NT, 6]), sb("work", [P, 4, NT])
        mean, rstd = sb("mean", [P, NT]), sb("rstd", [P, NT])
        xs = [sb(f"xs{i}", [P, T, P]) for i in range(2)]
        xT = [sb(f"xT{i}", [P, S]) for i in range(2)]
        zero = sb("zero", [P, S])
        logits, prob = sb("logits", [P, NT, E]), sb("prob", [P, NT, E])
        pairs = sb("pairs", [P, T, E, B])
        top, tot = sb("top", [P, NT]), sb("tot", [P, NT])
        cand = sb("cand", [ROWS, S])
        slots = sb("slots", [ROWS, CAP], U32)
        vals, toks = sb("vals", [ROWS, CAP]), sb("toks", [ROWS, CAP])
        psT = [ps(f"psT{i}", [P, S]) for i in range(2)]
        psL = ps("psL", [P, 512])
        psP = ps("psP", [ROWS, S])
        psI = ps("psI", [P, 512])
        s_var, s_std, s_dve = sem("var"), sem("std"), sem("dve")
        s_xs, s_xT, s_xTs, s_lg, s_lgs = sem("xs"), sem("xT"), sem("xT_sb"), sem("logits"), sem("logits_sb")
        s_xn = [sem(f"xn_dram{i}") for i in range(2)]
        s_zero, s_acc = sem("zero"), sem("acc_zeroed")
        s_sub, s_exp, s_prob, s_pT, s_list, s_lT = sem("sub"), sem("exp"), sem("prob"), sem("prob_T"), sem("list"), sem("list_T")
        xn_tiles = xn_dram.rearrange("(t p) c -> p t c", p=P)
        acc_tiles = acc_dram.rearrange("(t p) c -> p t c", p=P)

        net.raise_sems()
        with nc.Block() as block:
            @block.sync
            def _(sp):
                sp.wait_ge(s_zero, ONE + 1)
                for b in range(B):
                    sp.dma_start(acc_tiles[:, b * T:(b + 1) * T, :], zero[:].rearrange("p (t c) -> p t c", t=T)).then_inc(s_acc, 16)
                for b in range(B):
                    sp.wait_ge(s_xs, ONE + (b + 1) * T)
                    sp.dma_start(xn_tiles[:, b * T:(b + 1) * T, :], xs[b % 2][:]).then_inc(s_xn[b % 2], 16)
                for i in range(2):
                    sp.wait_ge(s_xn[i], ONE + 16 * B // 2)
                sp.wait_ge(s_acc, ONE + 16 * B)

            @block.tensor
            def _(pe):
                for b in range(B):
                    pe.wait_ge(s_xs, ONE + (b + 1) * T)
                    if b >= 2:
                        pe.wait_ge(s_xTs, ONE + b - 1)
                    for t in range(T):
                        last = pe.transpose(psT[b % 2][:, t * P:(t + 1) * P], xs[b % 2][:, t, :], w["ident"][:])
                    last.then_inc(s_xT, 1)
                    pe.wait_ge(s_xTs, ONE + b + 1)
                    if b:
                        pe.wait_ge(s_lgs, ONE + b)
                    for t in range(T):
                        last = pe.matmul(psL[:, t * E:(t + 1) * E], xT[b % 2][:, t * P:(t + 1) * P], w["gate"][:],
                                         start=True, stop=True)
                    last.then_inc(s_lg, 1)
                pe.wait_ge(s_prob, ONE + B)
                for t in range(T):
                    last = pe.transpose(psP[:, t * P:(t + 1) * P], pairs[:, t].rearrange("p e b -> p (e b)"),
                                        w["ident"][:])
                last.then_inc(s_pT, 1)
                pe.wait_ge(s_list, ONE + 1)
                for k, src in enumerate((vals, toks)):
                    for c in range(CH):
                        last = pe.transpose(psI[:, (k * CH + c) * ROWS:(k * CH + c + 1) * ROWS],
                                            src[:, c * P:(c + 1) * P], w["ident"][0:ROWS, 0:ROWS])
                last.then_inc(s_lT, 1)

            @block.scalar
            def _(act):
                act.wait_ge(s_var, ONE + 1)
                nc.scalar.activation(work[:, 2, :], work[:, 2, :], ACT.Sqrt).then_inc(s_std, 1)
                for b in range(B):
                    act.wait_ge(s_xT, ONE + b + 1)
                    if b >= 2:
                        act.wait_ge(s_lg, ONE + b - 1)
                    nc.scalar.activation(xT[b % 2][:], psT[b % 2][:], ACT.Copy).then_inc(s_xTs, 1)
                act.wait_ge(s_sub, ONE + 1)
                nc.scalar.activation(prob[:], prob[:], ACT.Exp).then_inc(s_exp, 1)

            @block.gpsimd
            def _(pool):
                nc.gpsimd.memset(zero[:], 0.0).then_inc(s_zero, 1)

            @block.vector
            def _(dve):
                done, var, std = Steps(s_dve), Steps(s_var), Steps(s_std)
                stats_of_x(net, dve, done, var, std, stats, work, mean[:], rstd[:])
                for b in range(B):
                    if b >= 2:
                        dve.wait_ge(s_xT, ONE + b - 1)
                        dve.wait_ge(s_xn[b % 2], ONE + 16 * (b // 2))
                    for t in range(T):
                        i = b * T + t
                        nc.vector.tensor_scalar(xs[b % 2][:, t, :], net.x[:, i, :], mean[:, i:i + 1], rstd[:, i:i + 1],
                                                op0=ALU.subtract, op1=ALU.mult).then_inc(s_xs, 1)
                for b in range(B):
                    dve.wait_ge(s_lg, ONE + b + 1)
                    nc.vector.tensor_copy(logits[:, b * T:(b + 1) * T, :].rearrange("p t e -> p (t e)"),
                                          psL[:, 0:T * E]).then_inc(s_lgs, 1)
                dve.wait_ge(s_lgs, ONE + B)
                done.step(nc.vector.reduce_max(top[:], logits[:], AX_X))
                dve.wait_ge(done.sem, done.at)
                nc.vector.tensor_tensor(prob[:], logits[:], top[:][:, :, None].to_broadcast([P, NT, E]),
                                        ALU.subtract).then_inc(s_sub, 1)
                dve.wait_ge(s_exp, ONE + 1)
                done.step(nc.vector.reduce_sum(tot[:], prob[:], AX_X))
                dve.wait_ge(done.sem, done.at)
                done.step(nc.vector.reciprocal(tot[:], tot[:]))
                dve.wait_ge(done.sem, done.at)
                for b in range(B):
                    rows = slice(b * T, (b + 1) * T)
                    nc.vector.tensor_tensor(pairs[:, :, :, b], prob[:, rows, :],
                                            tot[:, rows][:, :, None].to_broadcast([P, T, E]),
                                            ALU.mult).then_inc(s_prob, 1)
                dve.wait_ge(s_pT, ONE + 1)
                done.step(nc.vector.tensor_copy(cand[:], psP[:]))
                dve.wait_ge(done.sem, done.at)
                for r in range(ROUNDS):
                    k = slice(r * 8, (r + 1) * 8)
                    done.step(nc.vector.max(vals[:, k], cand[:]))
                    dve.wait_ge(done.sem, done.at)
                    done.step(nc.vector.max_index(slots[:, k], vals[:, k], cand[:]))
                    if r < ROUNDS - 1:
                        done.step(nc.vector.match_replace(cand[:], vals[:, k], cand[:], -1.0))
                        dve.wait_ge(done.sem, done.at)
                dve.wait_ge(done.sem, done.at)
                nc.vector.tensor_scalar(toks[:], slots[:], net.rowbase[:], None, op0=ALU.add).then_inc(s_list, 1)
                dve.wait_ge(s_lT, ONE + 1)
                n = CH * ROWS
                done.step(nc.vector.tensor_copy(weight[:].rearrange("p c r -> p (c r)"), psI[:, 0:n]))
                done.step(nc.vector.tensor_copy(idx[:].rearrange("p c r -> p (c r)"), psI[:, n:2 * n]))
                dve.wait_ge(done.sem, done.at)


def ffn_experts(net, acc_dram, xn_dram, idx, weight):
    nc, w = net.nc, net.w
    with ExitStack() as ctx:
        sb, ps, sem = net.makers(ctx)
        idx_e = sb("idx_e", [P, CH, B], U32)
        weight_e = sb("weight_e", [P, CH, B])
        xg = [sb(f"xg{b}", [P, CH, P]) for b in range(B)]
        xg_hi, xg_lo = [sb(f"xg_hi{i}", [P, CAP], F16) for i in range(2)], [sb(f"xg_lo{i}", [P, CAP], F16) for i in range(2)]
        hid = [sb(f"hid{i}", [P, FC, CAP]) for i in range(2)]
        y = [sb(f"y{b}", [P, CH, P]) for b in range(B)]
        accs = [sb(f"acc{b}", [P, T, P]) for b in range(B)]
        accb = [sb(f"accb{b}", [P, T, P], BF16) for b in range(B)]
        psX = ps("psX", [P, 512])
        psH = [ps(f"psH{i}", [P, FC * CAP]) for i in range(2)]
        psY = ps("psY", [P, 512])
        s_idx, s_wt, s_past = sem("idx_e"), sem("weight_e"), sem("pool_past_wait")
        s_xg = [sem(f"gathered{b}", swdge=True) for b in range(B)]
        s_sc = [sem(f"scattered{b}", swdge=True) for b in range(B)]
        s_free = sem("all_scattered")
        s_xT, s_xhi, s_xlo = sem("xg_T"), sem("xg_hi"), sem("xg_lo")
        s_h, s_gelu, s_y, s_ys = sem("h"), sem("gelu"), sem("y"), sem("y_sb")
        s_back, s_cast, s_added = [sem(f"acc_back{b}") for b in range(B)], sem("cast"), sem("added")
        acc_tiles = acc_dram.rearrange("(t p) c -> p t c", p=P)

        net.raise_sems()
        with nc.Block() as block:
            @block.gpsimd
            def _(pool):
                with pool.Fori(0, E) as e:
                    pool.wait_ge(s_idx, ONE + e + 1)
                    for b in range(B):
                        pool.wait_ge(s_xT, ONE + e * B)
                        pool.sem_inc(s_past, 1)
                        for c in range(CH):
                            pool.indirect_dma_start(xg[b][:, c, :], None, xn_dram,
                                                    bass.IndirectOffsetOnAxis(ap=idx_e[:, c, b:b + 1], axis=0)
                                                    ).then_inc(s_xg[b], 16)
                    for b in range(B):
                        pool.wait_ge(s_ys, ONE + e * B + b + 1)
                        pool.sem_inc(s_past, 1)
                        for c in range(CH):
                            pool.indirect_dma_start(acc_dram, bass.IndirectOffsetOnAxis(ap=idx_e[:, c, b:b + 1], axis=0),
                                                    y[b][:, c, :], None, compute_op=ALU.add).then_inc(s_sc[b], 16)
                    for b in range(B):
                        pool.wait_ge(s_sc[b], (e + 1) * 16 * CH)
                    pool.sem_inc(s_free, 1)

            @block.tensor
            def _(pe):
                with pe.Fori(0, E) as e:
                    def up(b):
                        u = e * B + b
                        pe.wait_ge(s_xg[b], (e + 1) * 16 * CH)
                        pe.wait_ge(s_xlo, ONE + u)
                        for c in range(CH):
                            last = pe.transpose(psX[:, c * P:(c + 1) * P], xg[b][:, c, :], w["ident"][:])
                        last.then_inc(s_xT, 1)
                        pe.wait_ge(s_xhi, ONE + u + 1)
                        pe.wait_ge(s_xlo, ONE + u + 1)
                        pe.wait_ge(s_gelu, ONE + u - 1) if b >= 1 else pe.wait_ge(s_gelu, ONE + e * B)
                        for f in range(FC):
                            cols = bass.ds(e * (FC * P) + f * P, P)
                            for i, (l, r) in enumerate(((net.hi["w1"], xg_hi), (net.hi["w1"], xg_lo), (net.lo["w1"], xg_hi))):
                                last = pe.matmul(psH[b % 2][:, f * CAP:(f + 1) * CAP], l[:, cols], r[b % 2][:],
                                                 start=(i == 0), stop=(i == 2))
                        last.then_inc(s_h, 1)

                    def down(b):
                        u = e * B + b
                        pe.wait_ge(s_gelu, ONE + u + 1)
                        pe.wait_ge(s_ys, ONE + u)
                        for c in range(CH):
                            for f in range(FC):
                                last = pe.matmul(psY[:, c * P:(c + 1) * P], hid[b % 2][:, f, c * P:(c + 1) * P],
                                                 w["w2"][:, bass.ds(e * (FC * P) + f * P, P)],
                                                 start=(f == 0), stop=(f == FC - 1))
                        last.then_inc(s_y, 1)

                    up(0)
                    for b in range(1, B):
                        up(b)
                        down(b - 1)
                    down(B - 1)

            @block.scalar
            def _(act):
                with act.Fori(0, E) as e:
                    def cast(b):
                        u = e * B + b
                        act.wait_ge(s_xT, ONE + u + 1)
                        act.wait_ge(s_h, ONE + u - 1) if b >= 1 else act.wait_ge(s_h, ONE + e * B)
                        nc.scalar.activation(xg_hi[b % 2][:], psX[:, 0:CAP], ACT.Copy).then_inc(s_xhi, 1)

                    def gelu(b):
                        u = e * B + b
                        act.wait_ge(s_h, ONE + u + 1)
                        act.wait_ge(s_y, ONE + u - 1) if b >= 1 else act.wait_ge(s_y, ONE + e * B)
                        nc.scalar.activation(hid[b % 2][:].rearrange("p f s -> p (f s)"), psH[b % 2][:],
                                             ACT.Gelu_apprx_tanh, scale=1.0 / WS).then_inc(s_gelu, 1)

                    cast(0)
                    for b in range(1, B):
                        cast(b)
                        gelu(b - 1)
                    gelu(B - 1)

            @block.vector
            def _(dve):
                with dve.Fori(0, E) as e:
                    dve.wait_ge(s_free, ONE + e)
                    nc.vector.tensor_copy(idx_e[:], idx[:, :, bass.ds(e * B, B)]).then_inc(s_idx, 1)
                    dve.wait_ge(s_ys, ONE + e * B)
                    nc.vector.tensor_copy(weight_e[:], weight[:, :, bass.ds(e * B, B)]).then_inc(s_wt, 1)

                    def low(b):
                        u = e * B + b
                        dve.wait_ge(s_xhi, ONE + u + 1)
                        nc.vector.tensor_tensor(xg_lo[b % 2][:], psX[:, 0:CAP], xg_hi[b % 2][:],
                                                ALU.subtract).then_inc(s_xlo, 1)

                    def weigh(b):
                        u = e * B + b
                        dve.wait_ge(s_y, ONE + u + 1)
                        dve.wait_ge(s_wt, ONE + e + 1)
                        nc.vector.tensor_tensor(y[b][:], psY[:, 0:CAP].rearrange("p (c d) -> p c d", c=CH),
                                                weight_e[:, :, b:b + 1].to_broadcast([P, CH, P]),
                                                ALU.mult).then_inc(s_ys, 1)

                    low(0)
                    for b in range(1, B):
                        low(b)
                        weigh(b - 1)
                    weigh(B - 1)
                for b in range(B):
                    dve.wait_ge(s_back[b], ONE + 16)
                    nc.vector.tensor_copy(accb[b][:], accs[b][:]).then_inc(s_cast, 1)
                    dve.wait_ge(s_cast, ONE + b + 1)
                    rows = net.x[:, b * T:(b + 1) * T, :]
                    nc.vector.tensor_tensor(rows, rows, accb[b][:], ALU.add).then_inc(s_added, 1)

            @block.sync
            def _(sp):
                for b in range(B):
                    sp.wait_ge(s_sc[b], E * 16 * CH)
                    sp.dma_start(accs[b][:], acc_tiles[:, b * T:(b + 1) * T, :]).then_inc(s_back[b], 16)


def attention_b(net):
    nc, w = net.nc, net.w
    UNITS = [(g, q) for g in range(GROUP) for q in range(T)]
    HALF = P // 2
    LAST = len(UNITS)
    with ExitStack() as ctx:
        sb, ps, sem = net.makers(ctx)
        stats, work = sb("stats", [P, NT, 6]), sb("work", [P, 4, NT])
        mean, rstd = sb("mean", [P, NT]), sb("rstd", [P, NT])
        xs = sb("xs", [P, T, P])
        xT_hi, xT_lo = sb("xT_hi", [P, S], F16), sb("xT_lo", [P, S], F16)
        qk = [sb(f"qk{i}", [P, S]) for i in range(GROUP + 1)]
        v = sb("v", [P, S])
        by_cos, by_sin = [sb(f"by_cos{i}", [P, S]) for i in range(2)], [sb(f"by_sin{i}", [P, S]) for i in range(2)]
        prob, probT = [sb(f"prob{i}", [P, S]) for i in range(2)], [sb(f"probT{i}", [P, S]) for i in range(2)]
        nmax, nbias, rowsum, rinv = (sb(n, [P, LAST]) for n in ("nmax", "nbias", "rowsum", "rinv"))
        oT = sb("oT", [P, NH, S])
        psS = [ps(f"psS{i}", [P, S]) for i in range(2)]
        psT = ps("psT", [P, S])
        psO = [ps(f"psO{i}", [P, 512]) for i in range(2)]
        s_var, s_std, s_dve = sem("var"), sem("std"), sem("dve")
        s_xs, s_xT, s_xhi, s_xlo = sem("xs"), sem("xT"), sem("x_hi"), sem("x_lo")
        s_proj, s_rope, s_rot, s_v = sem("proj"), sem("rope"), sem("rotated"), sem("v")
        s_s, s_nb, s_exp, s_p, s_pT, s_pTs = sem("scores"), sem("nbias"), sem("exp"), sem("p"), sem("p_T"), sem("pT_sb")
        s_o, s_os, s_y, s_ys = sem("o"), sem("oT_sb"), sem("y"), sem("y_added")
        QB = 512 // P
        NO = LAST // QB

        net.raise_sems()
        with nc.Block() as block:
            @block.tensor
            def _(pe):
                with pe.Fori(0, B) as b:
                    pe.wait_ge(s_xs, ONE + (b + 1) * T)
                    pe.wait_ge(s_ys, ONE + b)
                    for t in range(T):
                        last = pe.transpose(psT[:, t * P:(t + 1) * P], xs[:, t, :], w["ident"][:])
                    last.then_inc(s_xT, 1)
                    with pe.Fori(0, NKV) as j:
                        n = b * NKV + j
                        pe.wait_ge(s_xhi, ONE + b + 1)
                        pe.wait_ge(s_xlo, ONE + b + 1)
                        parts = (("hi", xT_hi), ("hi", xT_lo), ("lo", xT_hi))

                        def weights(key, part, cols):
                            return (net.hi if part == "hi" else net.lo)[key][:, cols]

                        pe.wait_ge(s_exp, ONE + n * LAST)
                        for i in range(GROUP + 1):
                            if i >= 2:
                                pe.wait_ge(s_rope, ONE + 3 * (n * (GROUP + 1) + i - 1))
                            key = "wk" if i == GROUP else "wq"
                            cols = bass.ds(j * P, P) if i == GROUP else bass.ds(j * (GROUP * P) + i * P, P)
                            for c in range(2):
                                half = slice(c * 512, (c + 1) * 512)
                                for k, (part, src) in enumerate(parts):
                                    last = pe.matmul(psS[i % 2][:, half], weights(key, part, cols), src[:, half],
                                                     start=(k == 0), stop=(k == 2))
                            last.then_inc(s_proj, 1)
                        pe.wait_ge(s_rope, ONE + 3 * (n * (GROUP + 1) + GROUP))
                        for t in range(T):
                            rows = slice(t * P, (t + 1) * P)
                            for k, (part, src) in enumerate((("hi", xT_hi), ("lo", xT_hi), ("hi", xT_lo))):
                                last = pe.matmul(psS[1][:, rows], src[:, rows], weights("wv", part, bass.ds(j * P, P)),
                                                 start=(k == 0), stop=(k == 2))
                        last.then_inc(s_proj, 1)

                        def scores(u):
                            g, q = UNITS[u]
                            if u >= 2:
                                pe.wait_ge(s_exp, ONE + n * LAST + u - 1)
                            width = (q + 1) * P
                            for c in range(0, width, 512):
                                end = min(width, c + 512)
                                last = pe.matmul(psS[u % 2][:, c:end], qk[g][:, q * P:(q + 1) * P], qk[GROUP][:, c:end],
                                                 start=True, stop=(end < width))
                            last = pe.matmul(psS[u % 2][:, q * P:width], w["identb"][:], w["maskb"][:],
                                             start=False, stop=True)
                            last.then_inc(s_s, 1)

                        def turn(u):
                            g, q = UNITS[u]
                            pe.wait_ge(s_p, ONE + n * LAST + u + 1)
                            pe.wait_ge(s_pTs, ONE + n * LAST + u)
                            for k in range(q + 1):
                                last = pe.transpose(psT[:, k * P:(k + 1) * P], prob[u % 2][:, k * P:(k + 1) * P],
                                                    w["ident"][:])
                            last.then_inc(s_pT, 1)

                        def values(u):
                            g, q = UNITS[u]
                            pe.wait_ge(s_pTs, ONE + n * LAST + u + 1)
                            if q % QB == 0:
                                o = u // QB
                                if o >= 2:
                                    pe.wait_ge(s_os, ONE + n * NO + o - 1)
                                else:
                                    pe.wait_ge(s_os, ONE + n * NO)
                            for k in range(q + 1):
                                last = pe.matmul(psO[u // QB % 2][:, q % QB * P:(q % QB + 1) * P],
                                                 v[:, k * P:(k + 1) * P], probT[u % 2][:, k * P:(k + 1) * P],
                                                 start=(k == 0), stop=(k == q))
                            last.then_inc(s_o, 1)

                        pe.wait_ge(s_rot, ONE + (n + 1) * (GROUP + 1))
                        scores(0)
                        pe.wait_ge(s_v, ONE + n + 1)
                        scores(1)
                        for u in range(LAST):
                            turn(u)
                            if u + 2 < LAST:
                                scores(u + 2)
                            if u >= 1:
                                values(u - 1)
                        values(LAST - 1)
                    pe.wait_ge(s_os, ONE + (b + 1) * (NKV * NO))
                    for t in range(T):
                        rows = slice(t * P, (t + 1) * P)
                        for h in range(NH):
                            last = pe.matmul(psT[:, rows], oT[:, h, rows], w["wo"][:, h * P:(h + 1) * P],
                                             start=(h == 0), stop=(h == NH - 1))
                    last.then_inc(s_y, 1)

            def finish(dve, n, u, done):
                g, q = UNITS[u]
                dve.wait_ge(s_exp, ONE + n * LAST + u + 1)
                done.step(nc.vector.reciprocal(rinv[:, u:u + 1], rowsum[:, u:u + 1]))
                dve.wait_ge(done.sem, done.at)
                p = prob[u % 2][:, 0:(q + 1) * P]
                nc.vector.tensor_scalar(p, p, rinv[:, u:u + 1], 1.0 / WS, op0=ALU.mult, op1=ALU.mult).then_inc(s_p, 1)

            @block.vector
            def _(dve):
                done, var, std = Steps(s_dve), Steps(s_var), Steps(s_std)
                stats_of_x(net, dve, done, var, std, stats, work, mean[:], rstd[:])
                with dve.Fori(0, B) as b:
                    dve.wait_ge(s_xT, ONE + b)
                    for t in range(T):
                        i = b * T + t
                        nc.vector.tensor_scalar(xs[:, t, :], net.x[:, bass.ds(i, 1), :].rearrange("p a b -> p (a b)"),
                                                mean[:, bass.ds(i, 1)], rstd[:, bass.ds(i, 1)],
                                                op0=ALU.subtract, op1=ALU.mult).then_inc(s_xs, 1)
                    dve.wait_ge(s_xhi, ONE + b + 1)
                    dve.wait_ge(s_proj, ONE + b * (NKV * (GROUP + 2)))
                    nc.vector.tensor_tensor(xT_lo[:], psT[:], xT_hi[:], ALU.subtract).then_inc(s_xlo, 1)
                    done.enter(b, NKV * 2 * LAST)
                    with dve.Fori(0, NKV) as j:
                        n = b * NKV + j
                        done.enter(j, 2 * LAST)
                        for i in range(GROUP + 1):
                            m = n * (GROUP + 1) + i
                            dve.wait_ge(s_proj, ONE + n * (GROUP + 2) + i + 1)
                            if i >= 2:
                                dve.wait_ge(s_rot, ONE + m - 1)
                            else:
                                dve.wait_ge(s_rot, ONE + n * (GROUP + 1))
                            src = psS[i % 2]
                            nc.vector.tensor_tensor(by_cos[i % 2][:], src[:], w["cos"][:], ALU.mult).then_inc(s_rope, 1)
                            for lo, hi in ((0, HALF), (HALF, 0)):
                                nc.vector.tensor_tensor(by_sin[i % 2][lo:lo + HALF, :], src[hi:hi + HALF, :],
                                                        w["sin"][hi:hi + HALF, :], ALU.mult).then_inc(s_rope, 1)

                        for u, (g, q) in enumerate(UNITS):
                            width = (q + 1) * P
                            dve.wait_ge(s_s, ONE + n * LAST + u + 1)
                            done.step(nc.vector.reduce_max(nmax[:, u:u + 1], psS[u % 2][:, 0:width], AX_X, negate=True))
                            dve.wait_ge(done.sem, done.at)
                            nc.vector.tensor_scalar(nbias[:, u:u + 1], nmax[:, u:u + 1], SCALE / (WS * WS), None,
                                                    op0=ALU.mult).then_inc(s_nb, 1)
                            if u >= 1:
                                finish(dve, n, u - 1, done)
                        finish(dve, n, LAST - 1, done)
                        done.leave(NKV)
                    done.leave(B)
                    dve.wait_ge(s_y, ONE + b + 1)
                    rows = net.x[:, bass.ds(b * T, T), :]
                    nc.vector.tensor_tensor(rows, psT[:].rearrange("p (t c) -> p t c", t=T), rows, ALU.add).then_inc(s_ys, 1)

            @block.gpsimd
            def _(pool):
                with pool.Fori(0, B * NKV) as n:
                    pool.wait_ge(s_s, ONE + n * LAST)
                    for i in range(GROUP + 1):
                        pool.wait_ge(s_rope, ONE + 3 * (n * (GROUP + 1) + i + 1))
                        nc.gpsimd.tensor_tensor(qk[i][:], by_cos[i % 2][:], by_sin[i % 2][:], ALU.add).then_inc(s_rot, 1)

            @block.scalar
            def _(act):
                act.wait_ge(s_var, ONE + 1)
                nc.scalar.activation(work[:, 2, :], work[:, 2, :], ACT.Sqrt).then_inc(s_std, 1)
                with act.Fori(0, B) as b:
                    act.wait_ge(s_xT, ONE + b + 1)
                    act.wait_ge(s_proj, ONE + b * (NKV * (GROUP + 2)))
                    nc.scalar.activation(xT_hi[:], psT[:], ACT.Copy).then_inc(s_xhi, 1)
                    with act.Fori(0, NKV) as j:
                        n = b * NKV + j
                        act.wait_ge(s_proj, ONE + (n + 1) * (GROUP + 2))
                        act.wait_ge(s_o, ONE + n * LAST)
                        nc.scalar.activation(v[:], psS[1][:], ACT.Copy).then_inc(s_v, 1)

                        def exp(u):
                            g, q = UNITS[u]
                            act.wait_ge(s_nb, ONE + n * LAST + u + 1)
                            if u >= 2:
                                act.wait_ge(s_pT, ONE + n * LAST + u - 1)
                            width = (q + 1) * P
                            nc.scalar.activation(prob[u % 2][:, 0:width], psS[u % 2][:, 0:width], ACT.Exp,
                                                 bias=nbias[:, u:u + 1], scale=SCALE / (WS * WS),
                                                 accum_out=rowsum[:, u:u + 1]).then_inc(s_exp, 1)

                        def take_probT(u):
                            g, q = UNITS[u]
                            act.wait_ge(s_pT, ONE + n * LAST + u + 1)
                            if u >= 2:
                                act.wait_ge(s_o, ONE + n * LAST + u - 1)
                            width = (q + 1) * P
                            nc.scalar.activation(probT[u % 2][:, 0:width], psT[:, 0:width], ACT.Copy).then_inc(s_pTs, 1)

                        def take_o(o):
                            g, q = UNITS[o * QB]
                            act.wait_ge(s_o, ONE + n * LAST + (o + 1) * QB)
                            if o == 0:
                                act.wait_ge(s_y, ONE + b)
                            nc.scalar.activation(oT[:, bass.ds(j * GROUP + g, 1), q * P:(q + QB) * P].rearrange("p a c -> p (a c)"),
                                                 psO[o % 2][:], ACT.Copy).then_inc(s_os, 1)

                        exp(0)
                        for u in range(LAST):
                            if u + 1 < LAST:
                                exp(u + 1)
                            take_probT(u)
                            if u > QB and u % QB == 1:
                                take_o(u // QB - 1)
                        take_o(NO - 1)



def build(nc, d, out):
    with ExitStack() as ctx:
        net = Net(nc, ctx)
        load_stage(net, d)
        attention_a(net)
        xn_dram = nc.dram_tensor("xn", (B * S, P), F32, kind="Internal").ap()
        acc_dram = [nc.dram_tensor(f"acc{i}", (B * S, P), F32, kind="Internal").ap() for i in range(2)]
        ffn(net, "ffn0", acc_dram[0], xn_dram)
        if STAGES > 2:
            attention_b(net)
        if STAGES > 3:
            ffn(net, "ffn0", acc_dram[1], xn_dram)
        with nc.Block() as block:
            s_out = net.sem(ctx, "out")

            @block.sync
            def _(sp):
                sp.dma_start(out.rearrange("(t p) c -> p t c", p=P), net.x[:]).then_inc(s_out, 16)
                sp.wait_ge(s_out, 16)


def kernel(**inputs):
    import ml_dtypes
    import numpy as np
    import concourse.bacc as bacc
    from concourse.bass_utils import run_bass_kernel_spmd

    a = {k: np.asarray(v) for k, v in inputs.items()}
    lay = np.ascontiguousarray
    wqkv = a["L0_attn_a_w_qkv"]
    arrays = {
        "x": lay(a["L0_attn_a_x"].reshape(B * S, P)),
        "wq_a": lay(wqkv[0:P]), "wk_a": lay(wqkv[P:2 * P]), "wv_aT": lay(wqkv[2 * P:].T),
        "wfc_T": lay(a["L0_attn_a_w_fc"].T),
        "bfc": lay(np.broadcast_to(a["L0_attn_a_b_fc"], (P, P))),
        "gamma": lay(np.broadcast_to(a["L0_attn_a_gamma"], (P, P))),
        "beta": lay(np.broadcast_to(a["L0_attn_a_beta"], (P, P))),
        "gate": a["L0_ffn_gate_w"],
        "wq": a["L0_attn_b_Wq"], "wk": a["L0_attn_b_Wk"], "wv": a["L0_attn_b_Wv"],
        "wo": lay(a["L0_attn_b_Wo"].reshape(NH, P, P).transpose(1, 0, 2).reshape(P, NH * P)),
        "w1": lay(a["L0_ffn_w1"].transpose(1, 0, 2).reshape(P, E * FC * P)),
        "w2": lay(a["L0_ffn_w2"].reshape(E, FC, P, P).transpose(2, 0, 1, 3).reshape(P, E * FC * P)),
    }
    half = np.arange(0, P, 2, dtype=np.float32) / np.float32(P)
    inv_freq = (np.float32(1.0) / np.power(np.float32(10000.0), half)).astype(np.float32)
    angle = np.outer(inv_freq, np.arange(S, dtype=np.float32)).astype(np.float32)
    arrays["cos"] = lay(np.concatenate([np.cos(angle)] * 2).astype(np.float32))
    arrays["sin"] = lay(np.concatenate([np.sin(angle), -np.sin(angle)]).astype(np.float32))
    arrays["ident"] = np.eye(P, dtype=np.float32)
    arrays["identb"] = np.eye(P, dtype=ml_dtypes.bfloat16)
    arrays["maskb"] = np.triu(np.full((P, P), -1e30, np.float32), 1).astype(ml_dtypes.bfloat16)
    arrays["rowbase"] = (np.arange(ROWS, dtype=np.float32) % B * S).reshape(ROWS, 1).astype(np.float32)
    nc = bacc.Bacc("TRN2", target_bir_lowering=False, num_devices=1)
    d = {k: nc.dram_tensor(f"in_{k}", v.shape, mybir.dt.from_np(v.dtype), kind="ExternalInput").ap()
         for k, v in arrays.items()}
    out = nc.dram_tensor("out", (B * S, P), F32, kind="ExternalOutput").ap()
    build(nc, d, out)
    r = run_bass_kernel_spmd(nc, [{f"in_{k}": v for k, v in arrays.items()}], core_ids=[0])
    return r.results[0]["out"].reshape(B, S, P)
```

```python
import concourse.bass as bass
from concourse import mybir
from contextlib import ExitStack

F32 = mybir.dt.float32
F16 = mybir.dt.float16
BF16 = mybir.dt.bfloat16
U32 = mybir.dt.uint32
ALU = mybir.AluOpType
ACT = mybir.ActivationFunctionType
AX_X = mybir.AxisListType.X

P = 128
B, S = 4, 1024
T = S // P
NT = B * T
NH, NKV = 8, 4
GROUP = NH // NKV
E = 8
FC = 4
CAP = 2 * S // E
CH = CAP // P
ROWS = E * B
SCALE = float(P) ** -0.5
EPS = 1e-5
ONE = 8
WS = 64.0


class Steps:

    def __init__(self, sem):
        self.sem, self.base, self.n, self.outer = sem, ONE, 0, []

    @property
    def at(self):
        return self.base + self.n

    def step(self, instruction, n=1):
        instruction.then_inc(self.sem, n)
        self.n += n
        return self.at

    def expect(self, n=1):
        self.n += n
        return self.at

    def enter(self, i, per):
        self.outer.append((self.base, self.n, per))
        self.base, self.n = self.base + self.n + i * per, 0

    def leave(self, rounds):
        base, n, per = self.outer.pop()
        assert self.n == per, (self.sem, self.n)
        self.base, self.n = base, n + rounds * per


def flat(ap):
    return ap.rearrange("p a b -> p (a b)")


class Net:

    def __init__(self, nc, ctx):
        self.nc, self.ctx = nc, ctx
        self.n = 0

    def sb(self, ctx, name, shape, dt=F32):
        self.n += 1
        return ctx.enter_context(self.nc.sbuf_tensor(f"{name}_{self.n}", shape, dt))

    def ps(self, ctx, name, shape, dt=F32):
        self.n += 1
        return ctx.enter_context(self.nc.psum_tensor(f"{name}_{self.n}", shape, dt))

    def sem(self, ctx, name):
        self.n += 1
        return ctx.enter_context(self.nc.semaphore(f"{name}_{self.n}"))

    def makers(self, ctx):
        self.stage_sems = []

        def sem(name, swdge=False):
            if swdge:
                return self.sem(ctx, name)
            self.stage_sems.append(self.sem(ctx, name))
            return self.stage_sems[-1]

        return (lambda *a: self.sb(ctx, *a)), (lambda *a: self.ps(ctx, *a)), sem

    def raise_sems(self):
        with self.nc.Block() as block:
            @block.sync
            def _(sp):
                for s in self.stage_sems:
                    sp.sem_inc(s, ONE)


def load_stage(net, d):
    nc, ctx = net.nc, net.ctx
    net.x = net.sb(ctx, "x", [P, NT, P])
    plain = {"wq_a": P, "wk_a": P, "wv_aT": P, "wfc_T": P, "bfc": P, "gamma": P, "beta": P, "gate": E,
             "wo": NH * P, "w2": E * FC * P, "cos": S, "sin": S, "ident": P, "identb": P, "maskb": P}
    net.w = {k: net.sb(ctx, k, [P, n], BF16 if k.endswith("b") and k != "gab" else F32) for k, n in plain.items()}
    net.rowbase = net.sb(ctx, "rowbase", [ROWS, 1])
    parts = {"w1": E * FC * P, "wq": NH * P, "wk": NKV * P, "wv": NKV * P}
    net.hi = {k: net.sb(ctx, k + "_hi", [P, n], F16) for k, n in parts.items()}
    net.lo = {k: net.sb(ctx, k + "_lo", [P, n], F16) for k, n in parts.items()}
    with ExitStack() as tmp:
        raw = {k: net.sb(tmp, k + "_raw", [P, n]) for k, n in parts.items()}
        s_raw = {k: net.sem(tmp, k + "_loaded") for k in parts}
        s_hi = net.sem(tmp, "hi_ready")
        s_rest = net.sem(tmp, "rest_loaded")
        with nc.Block() as block:
            @block.sync
            def _(sp):
                for k in parts:
                    sp.dma_start(raw[k][:], d[k]).then_inc(s_raw[k], 16)
                x_tiles = d["x"].rearrange("(t p) c -> p t c", p=P)
                n = 0
                for b in range(B):
                    sp.dma_start(net.x[:, b * T:(b + 1) * T, :], x_tiles[:, b * T:(b + 1) * T, :]).then_inc(s_rest, 16)
                    n += 16
                for k in plain:
                    sp.dma_start(net.w[k][:], d[k]).then_inc(s_rest, 16)
                    n += 16
                sp.dma_start(net.rowbase[:], d["rowbase"]).then_inc(s_rest, 16)
                sp.wait_ge(s_rest, n + 16)

            @block.scalar
            def _(act):
                for k in parts:
                    act.wait_ge(s_raw[k], 16)
                    nc.scalar.activation(net.hi[k][:], raw[k][:], ACT.Copy, scale=WS).then_inc(s_hi, 1)

            @block.vector
            def _(dve):
                for i, k in enumerate(parts):
                    dve.wait_ge(s_raw[k], 16)
                    dve.wait_ge(s_hi, i + 1)
                    nc.vector.scalar_tensor_tensor(net.lo[k][:], raw[k][:], WS, net.hi[k][:], ALU.mult, ALU.subtract)


def norm_stats(nc, dve, done, sem_var, sem_std, stats, work, mean, rstd, src, n, loop):
    loop(n, lambda i, k: nc.vector.bn_stats(stats[:, bass.ds(i, 1), :].rearrange("p a b -> p (a b)"), src(i)))
    dve.wait_ge(done.sem, done.at)
    me, mo, ve, vo = stats[:, :, 1], stats[:, :, 4], stats[:, :, 2], stats[:, :, 5]
    total, diff, var, sq = work[:, 0, :], work[:, 1, :], work[:, 2, :], work[:, 3, :]
    done.step(nc.vector.tensor_tensor(total, me, mo, ALU.add))
    done.step(nc.vector.tensor_tensor(diff, me, mo, ALU.subtract))
    done.step(nc.vector.tensor_tensor(var, ve, vo, ALU.add))
    dve.wait_ge(done.sem, done.at)
    done.step(nc.vector.tensor_scalar(mean, total, 0.5, None, op0=ALU.mult))
    done.step(nc.vector.tensor_tensor(sq, diff, diff, ALU.mult))
    dve.wait_ge(done.sem, done.at)
    done.step(nc.vector.tensor_scalar(sq, sq, 0.25, EPS, op0=ALU.mult, op1=ALU.add))
    dve.wait_ge(done.sem, done.at)
    sem_var.step(nc.vector.scalar_tensor_tensor(var, var, 1.0 / P, sq, ALU.mult, ALU.add))
    dve.wait_ge(sem_std.sem, sem_std.expect())
    done.step(nc.vector.reciprocal(rstd, var))
    dve.wait_ge(done.sem, done.at)


def stats_of_x(net, dve, done, s_var, s_std, stats, work, mean, rstd):
    nc = net.nc

    def loop(n, body):
        with dve.Fori(0, B) as b:
            for t in range(T):
                body(b * T + t, t).then_inc(done.sem, 1)
        done.expect(n)

    norm_stats(nc, dve, done, s_var, s_std, stats, work, mean, rstd,
               lambda i: net.x[:, bass.ds(i, 1), :].rearrange("p a b -> p (a b)"), NT, loop)


def attention_a(net):
    nc, w = net.nc, net.w
    with ExitStack() as ctx:
        sb, ps, sem = net.makers(ctx)
        stats = sb("stats", [P, NT, 6])
        work = sb("work", [P, 4, NT])
        mean, rstd = sb("mean", [P, NT]), sb("rstd", [P, NT])
        xs = sb("xs", [P, T, P])
        xT_hi, xT_lo = sb("xT_hi", [P, S], F16), sb("xT_lo", [P, S], F16)
        g_hi, g_lo = sb("g_hi", [P, P], F16), sb("g_lo", [P, P], F16)
        qg_hi, qg_lo = sb("qg_hi", [P, S], F16), sb("qg_lo", [P, S], F16)
        xsum, vsum, vsum_b, crow = sb("xsum", [P, 1]), sb("vsum", [P, 1]), sb("vsum_b", [P, P]), sb("crow", [P, P])
        prob = sb("prob", [P, 2, S])
        nmax, nbias = sb("nmax", [P, T]), sb("nbias", [P, T])
        rowsum, rinv, wsum = sb("rowsum", [P, T]), sb("rinv", [P, T]), sb("wsum", [P, T])
        h = sb("h", [P, T, P])
        hn = sb("hn", [P, T, P])
        hstats, hwork = sb("hstats", [P, T, 6]), sb("hwork", [P, 4, T])
        hmean, hrstd = sb("hmean", [P, T]), sb("hrstd", [P, T])
        psT = ps("psT", [P, S])
        psS = [ps(f"psS{i}", [P, S]) for i in range(2)]
        psC = ps("psC", [P, 512])

        s_var, s_std = sem("var"), sem("std")
        s_dve, s_pool = sem("dve"), sem("pool")
        s_g, s_ghi = sem("g"), sem("g_hi")
        s_xs, s_xT, s_xhi, s_xlo = sem("xs"), sem("xT"), sem("x_hi"), sem("x_lo")
        s_qg, s_qghi, s_qglo = sem("qg"), sem("qg_hi"), sem("qg_lo")
        s_xsum, s_v, s_vb, s_c = sem("xsum"), sem("v"), sem("v_b"), sem("c")
        s_s, s_nb, s_exp, s_hn, s_hvar, s_hstd = sem("scores"), sem("nbias"), sem("exp"), sem("hn"), sem("hvar"), sem("hstd")

        net.raise_sems()
        with nc.Block() as block:
            @block.tensor
            def _(pe):
                pe.matmul(psC[:, 0:P], w["wq_a"][:], w["wk_a"][:], start=True, stop=True).then_inc(s_g, 1)
                with pe.Fori(0, B) as b:
                    pe.wait_ge(s_xs, ONE + (b + 1) * T)
                    pe.wait_ge(s_qghi, ONE + b)
                    pe.wait_ge(s_qglo, ONE + b)
                    for t in range(T):
                        last = pe.transpose(psT[:, t * P:(t + 1) * P], xs[:, t, :], w["ident"][:])
                    last.then_inc(s_xT, 1)
                    pe.wait_ge(s_xsum, ONE + b + 1)
                    pe.matmul(psC[:, P:P + 1], w["wv_aT"][:], xsum[:], start=True, stop=True).then_inc(s_v, 1)
                    pe.wait_ge(s_vb, ONE + b + 1)
                    pe.matmul(psC[:, 2 * P:3 * P], vsum_b[:], w["wfc_T"][:], start=True, stop=True).then_inc(s_c, 1)
                    pe.wait_ge(s_xhi, ONE + b + 1)
                    pe.wait_ge(s_xlo, ONE + b + 1)
                    for c in range(2):
                        cols = slice(c * 512, (c + 1) * 512)
                        for i, (l, r) in enumerate(((g_hi, xT_hi), (g_hi, xT_lo), (g_lo, xT_hi))):
                            last = pe.matmul(psT[:, cols], l[:], r[:, cols], start=(i == 0), stop=(i == 2))
                    last.then_inc(s_qg, 1)
                    pe.wait_ge(s_qghi, ONE + b + 1)
                    pe.wait_ge(s_qglo, ONE + b + 1)
                    for t in range(T):
                        pe.wait_ge(s_exp, ONE + b * T + t - 1) if t >= 1 else pe.wait_ge(s_exp, ONE + b * T)
                        rows = slice(t * P, (t + 1) * P)
                        for c in range(2):
                            cols = slice(c * 512, (c + 1) * 512)
                            for i, (l, r) in enumerate(((qg_hi, xT_hi), (qg_hi, xT_lo), (qg_lo, xT_hi))):
                                last = pe.matmul(psS[t % 2][:, cols], l[:, rows], r[:, cols],
                                                 start=(i == 0), stop=(i == 2))
                        last.then_inc(s_s, 1)

            @block.vector
            def _(dve):
                done, var, std = Steps(s_dve), Steps(s_var), Steps(s_std)
                dve.wait_ge(s_g, ONE + 1)
                dve.wait_ge(s_ghi, ONE + 1)
                done.step(nc.vector.scalar_tensor_tensor(g_lo[:], psC[:, 0:P], WS, g_hi[:], ALU.mult, ALU.subtract))
                stats_of_x(net, dve, done, var, std, stats, work, mean[:], rstd[:])
                hvar, hstd = Steps(s_hvar), Steps(s_hstd)
                with dve.Fori(0, B) as b:
                    done.enter(b, 36)
                    hvar.enter(b, 1)
                    hstd.enter(b, 1)
                    dve.wait_ge(s_xT, ONE + b)
                    for t in range(T):
                        i = b * T + t
                        nc.vector.tensor_scalar(xs[:, t, :], net.x[:, bass.ds(i, 1), :].rearrange("p a b -> p (a b)"),
                                                mean[:, bass.ds(i, 1)], rstd[:, bass.ds(i, 1)],
                                                op0=ALU.subtract, op1=ALU.mult).then_inc(s_xs, 1)
                    dve.wait_ge(s_xT, ONE + b + 1)
                    nc.vector.reduce_sum(xsum[:], psT[:], AX_X).then_inc(s_xsum, 1)
                    dve.wait_ge(s_xhi, ONE + b + 1)
                    dve.wait_ge(s_s, ONE + b * T)
                    nc.vector.tensor_tensor(xT_lo[:], psT[:], xT_hi[:], ALU.subtract).then_inc(s_xlo, 1)
                    dve.wait_ge(s_v, ONE + b + 1)
                    done.step(nc.vector.tensor_copy(vsum[:], psC[:, P:P + 1]))
                    dve.wait_ge(done.sem, done.at)
                    nc.vector.tensor_copy(vsum_b[:], vsum[:].to_broadcast([P, P])).then_inc(s_vb, 1)
                    dve.wait_ge(s_c, ONE + b + 1)
                    done.step(nc.vector.tensor_copy(crow[:], psC[:, 2 * P:3 * P]))
                    dve.wait_ge(s_qg, ONE + b + 1)
                    dve.wait_ge(s_qghi, ONE + b + 1)
                    nc.vector.tensor_tensor(qg_lo[:], psT[:], qg_hi[:], ALU.subtract).then_inc(s_qglo, 1)
                    for t in range(T):
                        dve.wait_ge(s_s, ONE + b * T + t + 1)
                        done.step(nc.vector.reduce_max(nmax[:, t:t + 1], psS[t % 2][:], AX_X, negate=True))
                        dve.wait_ge(done.sem, done.at)
                        nc.vector.tensor_scalar(nbias[:, t:t + 1], nmax[:, t:t + 1], SCALE / WS, None,
                                                op0=ALU.mult).then_inc(s_nb, 1)
                    dve.wait_ge(s_exp, ONE + (b + 1) * T)
                    done.step(nc.vector.reciprocal(rinv[:], rowsum[:]))
                    dve.wait_ge(done.sem, done.at)
                    done.step(nc.vector.tensor_tensor(wsum[:], rinv[:], rowsum[:], ALU.mult))
                    dve.wait_ge(done.sem, done.at)
                    for t in range(T):
                        done.step(nc.vector.scalar_tensor_tensor(h[:, t, :], crow[:], wsum[:, t:t + 1], xs[:, t, :],
                                                                 ALU.mult, ALU.add))
                    dve.wait_ge(done.sem, done.at)
                    done.step(nc.vector.tensor_tensor(h[:], h[:], w["bfc"][:, None, :].to_broadcast([P, T, P]), ALU.add))
                    dve.wait_ge(done.sem, done.at)
                    def loop(n, body):
                        for t in range(n):
                            done.step(body(t, t))

                    norm_stats(nc, dve, done, hvar, hstd, hstats, hwork, hmean[:], hrstd[:],
                               lambda t: h[:, t, :], T, loop)
                    dve.wait_ge(s_pool, ONE + 3 * b)
                    for t in range(T):
                        nc.vector.tensor_scalar(hn[:, t, :], h[:, t, :], hmean[:, t:t + 1], hrstd[:, t:t + 1],
                                                op0=ALU.subtract, op1=ALU.mult).then_inc(s_hn, 1)
                    for steps in (done, hvar, hstd):
                        steps.leave(B)

            @block.scalar
            def _(act):
                act.wait_ge(s_g, ONE + 1)
                nc.scalar.activation(g_hi[:], psC[:, 0:P], ACT.Copy, scale=WS).then_inc(s_ghi, 1)
                act.wait_ge(s_var, ONE + 1)
                nc.scalar.activation(work[:, 2, :], work[:, 2, :], ACT.Sqrt).then_inc(s_std, 1)
                with act.Fori(0, B) as b:
                    act.wait_ge(s_xsum, ONE + b + 1)
                    act.wait_ge(s_s, ONE + b * T)
                    nc.scalar.activation(xT_hi[:], psT[:], ACT.Copy).then_inc(s_xhi, 1)
                    act.wait_ge(s_qg, ONE + b + 1)
                    nc.scalar.activation(qg_hi[:], psT[:], ACT.Copy).then_inc(s_qghi, 1)
                    for t in range(T):
                        act.wait_ge(s_nb, ONE + b * T + t + 1)
                        if t >= 2:
                            act.wait_ge(s_exp, ONE + b * T + t - 1)
                        else:
                            act.wait_ge(s_exp, ONE + b * T)
                        nc.scalar.activation(prob[:, t % 2, :], psS[t % 2][:], ACT.Exp, bias=nbias[:, t:t + 1],
                                             scale=SCALE / WS, accum_out=rowsum[:, t:t + 1]).then_inc(s_exp, 1)
                    act.wait_ge(s_hvar, ONE + b + 1)
                    nc.scalar.activation(hwork[:, 2, :], hwork[:, 2, :], ACT.Sqrt).then_inc(s_hstd, 1)

            @block.gpsimd
            def _(pool):
                with pool.Fori(0, B) as b:
                    rows = net.x[:, bass.ds(b * T, T), :]
                    pool.wait_ge(s_hn, ONE + (b + 1) * T)
                    nc.gpsimd.tensor_tensor(hn[:], hn[:], w["gamma"][:, None, :].to_broadcast([P, T, P]), ALU.mult).then_inc(s_pool, 1)
                    pool.wait_ge(s_pool, ONE + b * 3 + 1)
                    nc.gpsimd.tensor_tensor(hn[:], hn[:], w["beta"][:, None, :].to_broadcast([P, T, P]), ALU.add).then_inc(s_pool, 1)
                    pool.wait_ge(s_pool, ONE + b * 3 + 2)
                    nc.gpsimd.tensor_tensor(rows, rows, hn[:], ALU.add).then_inc(s_pool, 1)


def ffn(net, acc_dram, xn_dram):
    nc, w = net.nc, net.w
    with ExitStack() as outer:
        idx = net.sb(outer, "idx", [P, CH, ROWS], U32)
        weight = net.sb(outer, "weight", [P, CH, ROWS])
        ffn_route(net, acc_dram, xn_dram, idx, weight)
        ffn_experts(net, acc_dram, xn_dram, idx, weight)


def ffn_route(net, acc_dram, xn_dram, idx, weight):
    nc, w = net.nc, net.w
    ROUNDS = CAP // 8
    with ExitStack() as ctx:
        sb, ps, sem = net.makers(ctx)
        stats, work = sb("stats", [P, NT, 6]), sb("work", [P, 4, NT])
        mean, rstd = sb("mean", [P, NT]), sb("rstd", [P, NT])
        xs = [sb(f"xs{i}", [P, T, P]) for i in range(2)]
        xT = [sb(f"xT{i}", [P, S]) for i in range(2)]
        zero = sb("zero", [P, S])
        logits, prob = sb("logits", [P, NT, E]), sb("prob", [P, NT, E])
        pairs = sb("pairs", [P, T, E, B])
        top, tot = sb("top", [P, NT]), sb("tot", [P, NT])
        cand = sb("cand", [ROWS, S])
        slots = sb("slots", [ROWS, CAP], U32)
        vals, toks = sb("vals", [ROWS, CAP]), sb("toks", [ROWS, CAP])
        psT = [ps(f"psT{i}", [P, S]) for i in range(2)]
        psL = ps("psL", [P, 512])
        psP = ps("psP", [ROWS, S])
        psI = ps("psI", [P, 512])
        s_var, s_std, s_dve = sem("var"), sem("std"), sem("dve")
        s_xs, s_xT, s_xTs, s_lg, s_lgs = sem("xs"), sem("xT"), sem("xT_sb"), sem("logits"), sem("logits_sb")
        s_xn = [sem(f"xn_dram{i}") for i in range(2)]
        s_zero, s_acc = sem("zero"), sem("acc_zeroed")
        s_sub, s_exp, s_prob, s_pT, s_list, s_lT = sem("sub"), sem("exp"), sem("prob"), sem("prob_T"), sem("list"), sem("list_T")
        xn_tiles = xn_dram.rearrange("(t p) c -> p t c", p=P)
        acc_tiles = acc_dram.rearrange("(t p) c -> p t c", p=P)

        net.raise_sems()
        with nc.Block() as block:
            @block.sync
            def _(sp):
                sp.wait_ge(s_zero, ONE + 1)
                for b in range(B):
                    sp.dma_start(acc_tiles[:, b * T:(b + 1) * T, :], zero[:].rearrange("p (t c) -> p t c", t=T)).then_inc(s_acc, 16)
                for b in range(B):
                    sp.wait_ge(s_xs, ONE + (b + 1) * T)
                    sp.dma_start(xn_tiles[:, b * T:(b + 1) * T, :], xs[b % 2][:]).then_inc(s_xn[b % 2], 16)
                for i in range(2):
                    sp.wait_ge(s_xn[i], ONE + 16 * B // 2)
                sp.wait_ge(s_acc, ONE + 16 * B)

            @block.tensor
            def _(pe):
                for b in range(B):
                    pe.wait_ge(s_xs, ONE + (b + 1) * T)
                    if b >= 2:
                        pe.wait_ge(s_xTs, ONE + b - 1)
                    for t in range(T):
                        last = pe.transpose(psT[b % 2][:, t * P:(t + 1) * P], xs[b % 2][:, t, :], w["ident"][:])
                    last.then_inc(s_xT, 1)
                    pe.wait_ge(s_xTs, ONE + b + 1)
                    if b:
                        pe.wait_ge(s_lgs, ONE + b)
                    for t in range(T):
                        last = pe.matmul(psL[:, t * E:(t + 1) * E], xT[b % 2][:, t * P:(t + 1) * P], w["gate"][:],
                                         start=True, stop=True)
                    last.then_inc(s_lg, 1)
                pe.wait_ge(s_prob, ONE + B)
                for t in range(T):
                    last = pe.transpose(psP[:, t * P:(t + 1) * P], pairs[:, t].rearrange("p e b -> p (e b)"),
                                        w["ident"][:])
                last.then_inc(s_pT, 1)
                pe.wait_ge(s_list, ONE + 1)
                for k, src in enumerate((vals, toks)):
                    for c in range(CH):
                        last = pe.transpose(psI[:, (k * CH + c) * ROWS:(k * CH + c + 1) * ROWS],
                                            src[:, c * P:(c + 1) * P], w["ident"][0:ROWS, 0:ROWS])
                last.then_inc(s_lT, 1)

            @block.scalar
            def _(act):
                act.wait_ge(s_var, ONE + 1)
                nc.scalar.activation(work[:, 2, :], work[:, 2, :], ACT.Sqrt).then_inc(s_std, 1)
                for b in range(B):
                    act.wait_ge(s_xT, ONE + b + 1)
                    if b >= 2:
                        act.wait_ge(s_lg, ONE + b - 1)
                    nc.scalar.activation(xT[b % 2][:], psT[b % 2][:], ACT.Copy).then_inc(s_xTs, 1)
                act.wait_ge(s_sub, ONE + 1)
                nc.scalar.activation(prob[:], prob[:], ACT.Exp).then_inc(s_exp, 1)

            @block.gpsimd
            def _(pool):
                nc.gpsimd.memset(zero[:], 0.0).then_inc(s_zero, 1)

            @block.vector
            def _(dve):
                done, var, std = Steps(s_dve), Steps(s_var), Steps(s_std)
                stats_of_x(net, dve, done, var, std, stats, work, mean[:], rstd[:])
                for b in range(B):
                    if b >= 2:
                        dve.wait_ge(s_xT, ONE + b - 1)
                        dve.wait_ge(s_xn[b % 2], ONE + 16 * (b // 2))
                    for t in range(T):
                        i = b * T + t
                        nc.vector.tensor_scalar(xs[b % 2][:, t, :], net.x[:, i, :], mean[:, i:i + 1], rstd[:, i:i + 1],
                                                op0=ALU.subtract, op1=ALU.mult).then_inc(s_xs, 1)
                for b in range(B):
                    dve.wait_ge(s_lg, ONE + b + 1)
                    nc.vector.tensor_copy(logits[:, b * T:(b + 1) * T, :].rearrange("p t e -> p (t e)"),
                                          psL[:, 0:T * E]).then_inc(s_lgs, 1)
                dve.wait_ge(s_lgs, ONE + B)
                done.step(nc.vector.reduce_max(top[:], logits[:], AX_X))
                dve.wait_ge(done.sem, done.at)
                nc.vector.tensor_tensor(prob[:], logits[:], top[:][:, :, None].to_broadcast([P, NT, E]),
                                        ALU.subtract).then_inc(s_sub, 1)
                dve.wait_ge(s_exp, ONE + 1)
                done.step(nc.vector.reduce_sum(tot[:], prob[:], AX_X))
                dve.wait_ge(done.sem, done.at)
                done.step(nc.vector.reciprocal(tot[:], tot[:]))
                dve.wait_ge(done.sem, done.at)
                for b in range(B):
                    rows = slice(b * T, (b + 1) * T)
                    nc.vector.tensor_tensor(pairs[:, :, :, b], prob[:, rows, :],
                                            tot[:, rows][:, :, None].to_broadcast([P, T, E]),
                                            ALU.mult).then_inc(s_prob, 1)
                dve.wait_ge(s_pT, ONE + 1)
                done.step(nc.vector.tensor_copy(cand[:], psP[:]))
                dve.wait_ge(done.sem, done.at)
                for r in range(ROUNDS):
                    k = slice(r * 8, (r + 1) * 8)
                    done.step(nc.vector.max(vals[:, k], cand[:]))
                    dve.wait_ge(done.sem, done.at)
                    done.step(nc.vector.max_index(slots[:, k], vals[:, k], cand[:]))
                    if r < ROUNDS - 1:
                        done.step(nc.vector.match_replace(cand[:], vals[:, k], cand[:], -1.0))
                        dve.wait_ge(done.sem, done.at)
                dve.wait_ge(done.sem, done.at)
                nc.vector.tensor_scalar(toks[:], slots[:], net.rowbase[:], None, op0=ALU.add).then_inc(s_list, 1)
                dve.wait_ge(s_lT, ONE + 1)
                n = CH * ROWS
                done.step(nc.vector.tensor_copy(weight[:].rearrange("p c r -> p (c r)"), psI[:, 0:n]))
                done.step(nc.vector.tensor_copy(idx[:].rearrange("p c r -> p (c r)"), psI[:, n:2 * n]))
                dve.wait_ge(done.sem, done.at)


def ffn_experts(net, acc_dram, xn_dram, idx, weight):
    nc, w = net.nc, net.w
    with ExitStack() as ctx:
        sb, ps, sem = net.makers(ctx)
        idx_e = sb("idx_e", [P, CH, B], U32)
        weight_e = sb("weight_e", [P, CH, B])
        xg = [sb(f"xg{b}", [P, CH, P]) for b in range(B)]
        xg_hi, xg_lo = [sb(f"xg_hi{i}", [P, CAP], F16) for i in range(2)], [sb(f"xg_lo{i}", [P, CAP], F16) for i in range(2)]
        hid = [sb(f"hid{i}", [P, FC, CAP]) for i in range(2)]
        y = [sb(f"y{b}", [P, CH, P]) for b in range(B)]
        accs = [sb(f"acc{b}", [P, T, P]) for b in range(B)]
        accb = [sb(f"accb{b}", [P, T, P], BF16) for b in range(B)]
        psX = ps("psX", [P, 512])
        psH = [ps(f"psH{i}", [P, FC * CAP]) for i in range(2)]
        psY = ps("psY", [P, 512])
        s_idx, s_wt, s_past = sem("idx_e"), sem("weight_e"), sem("pool_past_wait")
        s_xg = [sem(f"gathered{b}", swdge=True) for b in range(B)]
        s_sc = [sem(f"scattered{b}", swdge=True) for b in range(B)]
        s_free = sem("all_scattered")
        s_xT, s_xhi, s_xlo = sem("xg_T"), sem("xg_hi"), sem("xg_lo")
        s_h, s_gelu, s_y, s_ys = sem("h"), sem("gelu"), sem("y"), sem("y_sb")
        s_back, s_cast, s_added = [sem(f"acc_back{b}") for b in range(B)], sem("cast"), sem("added")
        acc_tiles = acc_dram.rearrange("(t p) c -> p t c", p=P)

        net.raise_sems()
        with nc.Block() as block:
            @block.gpsimd
            def _(pool):
                with pool.Fori(0, E) as e:
                    pool.wait_ge(s_idx, ONE + e + 1)
                    for b in range(B):
                        pool.wait_ge(s_xT, ONE + e * B)
                        pool.sem_inc(s_past, 1)
                        for c in range(CH):
                            pool.indirect_dma_start(xg[b][:, c, :], None, xn_dram,
                                                    bass.IndirectOffsetOnAxis(ap=idx_e[:, c, b:b + 1], axis=0)
                                                    ).then_inc(s_xg[b], 16)
                    for b in range(B):
                        pool.wait_ge(s_ys, ONE + e * B + b + 1)
                        pool.sem_inc(s_past, 1)
                        for c in range(CH):
                            pool.indirect_dma_start(acc_dram, bass.IndirectOffsetOnAxis(ap=idx_e[:, c, b:b + 1], axis=0),
                                                    y[b][:, c, :], None, compute_op=ALU.add).then_inc(s_sc[b], 16)
                    for b in range(B):
                        pool.wait_ge(s_sc[b], (e + 1) * 16 * CH)
                    pool.sem_inc(s_free, 1)

            @block.tensor
            def _(pe):
                with pe.Fori(0, E) as e:
                    def up(b):
                        u = e * B + b
                        pe.wait_ge(s_xg[b], (e + 1) * 16 * CH)
                        pe.wait_ge(s_xlo, ONE + u)
                        for c in range(CH):
                            last = pe.transpose(psX[:, c * P:(c + 1) * P], xg[b][:, c, :], w["ident"][:])
                        last.then_inc(s_xT, 1)
                        pe.wait_ge(s_xhi, ONE + u + 1)
                        pe.wait_ge(s_xlo, ONE + u + 1)
                        pe.wait_ge(s_gelu, ONE + u - 1) if b >= 1 else pe.wait_ge(s_gelu, ONE + e * B)
                        for f in range(FC):
                            cols = bass.ds(e * (FC * P) + f * P, P)
                            for i, (l, r) in enumerate(((net.hi["w1"], xg_hi), (net.hi["w1"], xg_lo), (net.lo["w1"], xg_hi))):
                                last = pe.matmul(psH[b % 2][:, f * CAP:(f + 1) * CAP], l[:, cols], r[b % 2][:],
                                                 start=(i == 0), stop=(i == 2))
                        last.then_inc(s_h, 1)

                    def down(b):
                        u = e * B + b
                        pe.wait_ge(s_gelu, ONE + u + 1)
                        pe.wait_ge(s_ys, ONE + u)
                        for c in range(CH):
                            for f in range(FC):
                                last = pe.matmul(psY[:, c * P:(c + 1) * P], hid[b % 2][:, f, c * P:(c + 1) * P],
                                                 w["w2"][:, bass.ds(e * (FC * P) + f * P, P)],
                                                 start=(f == 0), stop=(f == FC - 1))
                        last.then_inc(s_y, 1)

                    up(0)
                    for b in range(1, B):
                        up(b)
                        down(b - 1)
                    down(B - 1)

            @block.scalar
            def _(act):
                with act.Fori(0, E) as e:
                    def cast(b):
                        u = e * B + b
                        act.wait_ge(s_xT, ONE + u + 1)
                        act.wait_ge(s_h, ONE + u - 1) if b >= 1 else act.wait_ge(s_h, ONE + e * B)
                        nc.scalar.activation(xg_hi[b % 2][:], psX[:, 0:CAP], ACT.Copy).then_inc(s_xhi, 1)

                    def gelu(b):
                        u = e * B + b
                        act.wait_ge(s_h, ONE + u + 1)
                        act.wait_ge(s_y, ONE + u - 1) if b >= 1 else act.wait_ge(s_y, ONE + e * B)
                        nc.scalar.activation(hid[b % 2][:].rearrange("p f s -> p (f s)"), psH[b % 2][:],
                                             ACT.Gelu_apprx_tanh, scale=1.0 / WS).then_inc(s_gelu, 1)

                    cast(0)
                    for b in range(1, B):
                        cast(b)
                        gelu(b - 1)
                    gelu(B - 1)

            @block.vector
            def _(dve):
                with dve.Fori(0, E) as e:
                    dve.wait_ge(s_free, ONE + e)
                    nc.vector.tensor_copy(idx_e[:], idx[:, :, bass.ds(e * B, B)]).then_inc(s_idx, 1)
                    dve.wait_ge(s_ys, ONE + e * B)
                    nc.vector.tensor_copy(weight_e[:], weight[:, :, bass.ds(e * B, B)]).then_inc(s_wt, 1)

                    def low(b):
                        u = e * B + b
                        dve.wait_ge(s_xhi, ONE + u + 1)
                        nc.vector.tensor_tensor(xg_lo[b % 2][:], psX[:, 0:CAP], xg_hi[b % 2][:],
                                                ALU.subtract).then_inc(s_xlo, 1)

                    def weigh(b):
                        u = e * B + b
                        dve.wait_ge(s_y, ONE + u + 1)
                        dve.wait_ge(s_wt, ONE + e + 1)
                        nc.vector.tensor_tensor(y[b][:], psY[:, 0:CAP].rearrange("p (c d) -> p c d", c=CH),
                                                weight_e[:, :, b:b + 1].to_broadcast([P, CH, P]),
                                                ALU.mult).then_inc(s_ys, 1)

                    low(0)
                    for b in range(1, B):
                        low(b)
                        weigh(b - 1)
                    weigh(B - 1)
                for b in range(B):
                    dve.wait_ge(s_back[b], ONE + 16)
                    nc.vector.tensor_copy(accb[b][:], accs[b][:]).then_inc(s_cast, 1)
                    dve.wait_ge(s_cast, ONE + b + 1)
                    rows = net.x[:, b * T:(b + 1) * T, :]
                    nc.vector.tensor_tensor(rows, rows, accb[b][:], ALU.add).then_inc(s_added, 1)

            @block.sync
            def _(sp):
                for b in range(B):
                    sp.wait_ge(s_sc[b], E * 16 * CH)
                    sp.dma_start(accs[b][:], acc_tiles[:, b * T:(b + 1) * T, :]).then_inc(s_back[b], 16)


def attention_b(net):
    nc, w = net.nc, net.w
    PAIRS = GROUP * T // 2
    PROJ = GROUP + 2
    HEAD = [("pair", 0), ("pair", 1), ("proj", 0), ("pair", 2), ("pair", 3), ("proj", 1),
            ("pair", 4), ("pair", 5), ("proj", 2), ("pair", 6), ("pair", 7), ("proj", 3)]
    STEPS, LOOK = NKV * len(HEAD), 2
    NP = NKV * PAIRS
    SLOTS = {k - PROJ: ("proj", k) for k in range(PROJ)}
    for k in range(STEPS + LOOK):
        kind, i = HEAD[k % len(HEAD)]
        j = k // len(HEAD)
        SLOTS[k] = (kind, j * PAIRS + i if kind == "pair" else (j + 1) * PROJ + i)
    HALF = P // 2
    CHUNKS = 3
    with ExitStack() as ctx:
        sb, ps, sem = net.makers(ctx)
        stats, work = sb("stats", [P, NT, 6]), sb("work", [P, 4, NT])
        mean, rstd = sb("mean", [P, NT]), sb("rstd", [P, NT])
        xT_hi, xT_lo = sb("xT_hi", [P, (B + 1) * S], F16), sb("xT_lo", [P, (B + 1) * S], F16)
        qk_hi = [[sb(f"qk_hi{r}{i}", [P, S], F16) for i in range(GROUP + 1)] for r in range(2)]
        qk_lo = [[sb(f"qk_lo{r}{i}", [P, S], F16) for i in range(GROUP + 1)] for r in range(2)]
        v = [sb(f"v{r}", [P, S]) for r in range(2)]
        by_cos, by_sin = [sb(f"by_cos{i}", [P, S]) for i in range(2)], [sb(f"by_sin{i}", [P, S]) for i in range(2)]
        prob = [[sb(f"prob{z}{r}", [P, S // (1 + z)]) for r in range(2)] for z in range(2)]
        probT = [[sb(f"probT{z}{r}", [P, S // (1 + z)]) for r in range(2)] for z in range(2)]
        nmax, nbias, rowsum, rinv = (sb(n, [P, 2, NP]) for n in ("nmax", "nbias", "rowsum", "rinv"))
        oT = sb("oT", [P, NH, T, P])
        psS = [ps(f"psS{i}", [P, S]) for i in range(2)]
        psM = ps("psM", [P, 512])
        psT = ps("psT", [P, S])
        psO = ps("psO", [P, 512])
        s_var, s_std, s_dve = sem("var"), sem("std"), sem("dve")
        s_xs, s_xT, s_xhi, s_xlo = sem("xs"), sem("xT"), sem("x_hi"), sem("x_lo")
        s_slot = sem("slot_written")
        s_rope, s_rot, s_rsum, s_v = sem("roped"), sem("rotated"), sem("rot_sum"), sem("v")
        s_s, s_nb, s_exp, s_p = ([sem(f"{n}{z}") for z in range(2)] for n in ("scores", "nbias", "exp", "p"))
        s_T, s_Ts, s_o, s_os, s_y, s_ys = sem("p_T"), sem("pT_sb"), sem("o"), sem("oT_sb"), sem("y"), sem("y_added")

        def unit(a, z):
            m = a % (T // 2)
            return a % PAIRS // (T // 2), (T - 1 - m if z == 0 else m), a // PAIRS

        def score_bank(k, z):
            return psM if z else psS[k % 2]

        def slot_of(a):
            return a // PAIRS * len(HEAD) + (0, 1, 3, 4, 6, 7, 9, 10)[a % PAIRS]

        def until(eng, s, b, per, n):
            if isinstance(b, int) and b * per + n <= 0:
                return
            eng.wait_ge(s, ONE + b * per + n)

        def pe_scores(pe, b, a, z):
            g, q, j = unit(a, z)
            r, width, k = j % 2, (q + 1) * P, slot_of(a)
            bank, rows = score_bank(k, z), slice(q * P, (q + 1) * P)
            if z:
                until(pe, s_exp[1], b, NP, a)
            if a % (T // 2) == 0:
                until(pe, s_rot, b, NKV * (GROUP + 1), j * (GROUP + 1) + 2 + g)
            for c in range(0, width, 512):
                end = min(width, c + 512)
                for i, (l, rr) in enumerate(((qk_hi, qk_hi), (qk_hi, qk_lo), (qk_lo, qk_hi))):
                    last = pe.matmul(bank[:, c:end], l[r][1 + g][:, rows], rr[r][0][:, c:end],
                                     start=(i == 0), stop=(i == 2 and end < width))
            last = pe.matmul(bank[:, q * P:width], w["identb"][:], w["maskb"][:], start=False, stop=True)
            last.then_inc(s_s[z], 1)

        def pe_proj(pe, b, k, n):
            j, i = divmod(n, PROJ)
            parts = (("hi", xT_hi), ("hi", xT_lo), ("lo", xT_hi))
            seq, j = (b + 1, 0) if j == NKV else (b, j)
            bank = psS[k % 2]
            if i < GROUP + 1:
                key, col = ("wk", j * P) if i == 0 else ("wq", (j * GROUP + i - 1) * P)
                for c in range(2):
                    cols = bass.ds(seq * S + c * 512, 512)
                    for m, (part, src) in enumerate(parts):
                        wt = (net.hi if part == "hi" else net.lo)[key]
                        last = pe.matmul(bank[:, c * 512:(c + 1) * 512], wt[:, col:col + P], src[:, cols],
                                         start=(m == 0), stop=(m == 2))
            else:
                for t in range(T):
                    for m, (part, src) in enumerate(parts):
                        wt = (net.hi if part == "hi" else net.lo)["wv"]
                        last = pe.matmul(bank[:, t * P:(t + 1) * P], src[:, bass.ds(seq * S + t * P, P)],
                                         wt[:, j * P:(j + 1) * P], start=(m == 0), stop=(m == 2))
            last.then_inc(s_slot, 1)

        def pe_write(pe, b, k):
            kind, n = SLOTS[k]
            if k - 2 >= -PROJ:
                before, m = SLOTS[k - 2]
                if before == "pair":
                    until(pe, s_exp[0], b, NP, m + 1)
                elif m % PROJ < GROUP + 1:
                    until(pe, s_rope, b, 3 * NKV * (GROUP + 1), 3 * (m // PROJ * (GROUP + 1) + m % PROJ + 1))
                else:
                    until(pe, s_v, b, NKV, m // PROJ + 1)
            if kind == "pair":
                pe_scores(pe, b, n, 0)
            else:
                pe_proj(pe, b, k, n)

        def pe_turn(pe, b, a, z):
            g, q, j = unit(a, z)
            until(pe, s_p[z], b, NP, a + 1)
            for c in range(0, q + 1, 4):
                n = CHUNKS * a + (2 if z else c // 4)
                until(pe, s_Ts, b, CHUNKS * NP, n - 1)
                for i in range(c, min(q + 1, c + 4)):
                    at = n % 2 * 512 + (i - c) * P
                    last = pe.transpose(psT[:, at:at + P], prob[z][a % 2][:, i * P:(i + 1) * P], w["ident"][:])
                last.then_inc(s_T, 1)

        def pe_values(pe, b, a, z):
            g, q, j = unit(a, z)
            until(pe, s_Ts, b, CHUNKS * NP, CHUNKS * a + (3 if z else 2))
            if not z:
                until(pe, s_os, b, NP, a)
                if a % PAIRS == 0:
                    until(pe, s_v, b, NKV, j + 1)
            for i in range(q + 1):
                last = pe.matmul(psO[:, (1 - z) * P:(2 - z) * P], v[j % 2][:, i * P:(i + 1) * P],
                                 probT[z][a % 2][:, i * P:(i + 1) * P], start=(i == 0), stop=(i == q))
            last.then_inc(s_o, 1)

        def xs_of(b):
            return by_cos[b % 2]

        def dve_xT_low(dve, b):
            dve.wait_ge(s_xhi, ONE + b + 1)
            nc.vector.tensor_tensor(xT_lo[:, b * S:(b + 1) * S], psT[:], xT_hi[:, b * S:(b + 1) * S],
                                    ALU.subtract).then_inc(s_xlo, 1)

        def dve_rope(dve, b, k, n):
            j, i = divmod(n, PROJ)
            m = j * (GROUP + 1) + i
            until(dve, s_slot, b, NKV * PROJ, n + 1)
            until(dve, s_rot, b, NKV * (GROUP + 1), m - 1)
            src = psS[k % 2]
            nc.vector.tensor_tensor(by_cos[m % 2][:], src[:], w["cos"][:], ALU.mult).then_inc(s_rope, 1)
            for lo, hi in ((0, HALF), (HALF, 0)):
                nc.vector.tensor_tensor(by_sin[m % 2][lo:lo + HALF, :], src[hi:hi + HALF, :], w["sin"][hi:hi + HALF, :],
                                        ALU.mult).then_inc(s_rope, 1)

        def dve_max(dve, b, a, z, done):
            g, q, j = unit(a, z)
            until(dve, s_s[z], b, NP, a + 1)
            done.step(nc.vector.reduce_max(nmax[:, z, a % NP:a % NP + 1], score_bank(slot_of(a), z)[:, 0:(q + 1) * P], AX_X,
                                           negate=True))
            dve.wait_ge(done.sem, done.at)
            nc.vector.tensor_scalar(nbias[:, z, a % NP:a % NP + 1], nmax[:, z, a % NP:a % NP + 1], SCALE / (WS * WS), None,
                                    op0=ALU.mult).then_inc(s_nb[z], 1)

        def dve_divide(dve, b, a, z, done):
            g, q, j = unit(a, z)
            until(dve, s_exp[z], b, NP, a + 1)
            done.step(nc.vector.reciprocal(rinv[:, z, a % NP:a % NP + 1], rowsum[:, z, a % NP:a % NP + 1]))
            dve.wait_ge(done.sem, done.at)
            p = prob[z][a % 2][:, 0:(q + 1) * P]
            nc.vector.tensor_scalar(p, p, rinv[:, z, a % NP:a % NP + 1], 1.0 / WS, op0=ALU.mult, op1=ALU.mult).then_inc(s_p[z], 1)

        def dve_take(dve, b, k, done):
            kind, n = SLOTS[k]
            if kind == "pair":
                dve_max(dve, b, n, 0, done)
            elif n % PROJ < GROUP + 1:
                dve_rope(dve, b, k, n)

        def act_exp(act, b, a, z):
            g, q, j = unit(a, z)
            until(act, s_nb[z], b, NP, a + 1)
            until(act, s_T, b, CHUNKS * NP, CHUNKS * (a - 2) + (3 if z else 2))
            width = (q + 1) * P
            nc.scalar.activation(prob[z][a % 2][:, 0:width], score_bank(slot_of(a), z)[:, 0:width], ACT.Exp,
                                 bias=nbias[:, z, a % NP:a % NP + 1], scale=SCALE / (WS * WS),
                                 accum_out=rowsum[:, z, a % NP:a % NP + 1]).then_inc(s_exp[z], 1)

        def act_take(act, b, k):
            kind, n = SLOTS[k]
            if kind == "pair":
                act_exp(act, b, n, 0)
            elif n % PROJ == GROUP + 1:
                until(act, s_slot, b, NKV * PROJ, n + 1)
                j = n // PROJ
                until(act, s_o, b, 2 * NP, 2 * PAIRS * (j - 1))
                nc.scalar.activation(v[j % 2][:], psS[k % 2][:], ACT.Copy).then_inc(s_v, 1)

        def act_probT(act, b, a, z):
            g, q, j = unit(a, z)
            for c in range(0, q + 1, 4):
                n = CHUNKS * a + (2 if z else c // 4)
                until(act, s_T, b, CHUNKS * NP, n + 1)
                width = (min(q + 1, c + 4) - c) * P
                until(act, s_o, b, 2 * NP, 2 * (a - 2) + 1 + z)
                nc.scalar.activation(probT[z][a % 2][:, c * P:c * P + width], psT[:, n % 2 * 512:n % 2 * 512 + width],
                                     ACT.Copy).then_inc(s_Ts, 1)

        def act_oT(act, b, a):
            g, q, j = unit(a, 1)
            until(act, s_o, b, 2 * NP, 2 * a + 2)
            if a == 0:
                until(act, s_y, b, 2, 0)
            out = oT[:, j * GROUP + g, q:T - q:T - 1 - 2 * q, :]
            nc.scalar.activation(out, psO[:, 0:2 * P].rearrange("p (z c) -> p z c", z=2), ACT.Copy).then_inc(s_os, 1)

        net.raise_sems()
        with nc.Block() as block:
            @block.tensor
            def _(pe):
                for b in range(B):
                    pe.wait_ge(s_xs, ONE + (b + 1) * T)
                    pe.wait_ge(s_xlo, ONE + 1 + b)
                    for t in range(T):
                        last = pe.transpose(psT[:, t * P:(t + 1) * P], xs_of(b)[:, t * P:(t + 1) * P], w["ident"][:])
                    last.then_inc(s_xT, 1)
                pe.wait_ge(s_xlo, ONE + B + 1)
                for k in range(-PROJ, LOOK):
                    pe_write(pe, 0, k)
                pe_scores(pe, 0, 0, 1)
                with pe.Fori(0, B) as b:
                    for k in range(STEPS):
                        kind, a = SLOTS[k]
                        if kind == "pair":
                            if a == 0:
                                until(pe, s_ys, b, 2, 0)
                            pe_turn(pe, b, a, 0)
                            pe_scores(pe, b, a + 1, 1)
                        pe_write(pe, b, k + LOOK)
                        if kind == "pair":
                            pe_turn(pe, b, a, 1)
                            pe_values(pe, b, a, 0)
                            pe_values(pe, b, a, 1)
                    until(pe, s_os, b, NP, NP)
                    until(pe, s_Ts, b, CHUNKS * NP, CHUNKS * NP)
                    for t in range(T):
                        for h in range(NH):
                            last = pe.matmul(psT[:, t * P:(t + 1) * P], oT[:, h, t, :], w["wo"][:, h * P:(h + 1) * P],
                                             start=(h == 0), stop=(h == NH - 1))
                        if t % 4 == 3:
                            last.then_inc(s_y, 1)

            @block.vector
            def _(dve):
                done, var, std = Steps(s_dve), Steps(s_var), Steps(s_std)
                nc.vector.memset(xT_hi[:, B * S:], 0.0).then_inc(s_xlo, 1)
                nc.vector.memset(xT_lo[:, B * S:], 0.0).then_inc(s_dve, 1)
                done.expect()
                stats_of_x(net, dve, done, var, std, stats, work, mean[:], rstd[:])
                for b in range(B):
                    if b >= 2:
                        dve.wait_ge(s_xT, ONE + b - 1)
                    for t in range(T):
                        i = b * T + t
                        nc.vector.tensor_scalar(xs_of(b)[:, t * P:(t + 1) * P], net.x[:, i, :], mean[:, i:i + 1],
                                                rstd[:, i:i + 1], op0=ALU.subtract, op1=ALU.mult).then_inc(s_xs, 1)
                    if b:
                        dve_xT_low(dve, b - 1)
                dve_xT_low(dve, B - 1)
                for k in range(-PROJ, LOOK):
                    dve_take(dve, 0, k, done)
                dve_max(dve, 0, 0, 1, done)
                dve_divide(dve, 0, 0, 0, done)
                with dve.Fori(0, B) as b:
                    done.enter(b, 4 * NP)
                    for k in range(STEPS):
                        kind, a = SLOTS[k]
                        if kind == "pair":
                            dve_divide(dve, b, a, 1, done)
                        if SLOTS[k + 1][0] == "pair":
                            dve_divide(dve, b, SLOTS[k + 1][1], 0, done)
                        if kind == "pair":
                            dve_max(dve, b, a + 1, 1, done)
                        dve_take(dve, b, k + LOOK, done)
                    done.leave(B)
                    for c in range(2):
                        until(dve, s_y, b, 2, c + 1)
                        rows = net.x[:, bass.ds(b * T + c * 4, 4), :]
                        nc.vector.tensor_tensor(rows, psT[:, c * 512:(c + 1) * 512].rearrange("p (t c) -> p t c", t=4), rows,
                                                ALU.add).then_inc(s_ys, 1)

            @block.gpsimd
            def _(pool):
                R = GROUP + 1

                def rotate(n, i, r):
                    m = (r * R + i) % 2
                    cos, sin, hi, lo = by_cos[m], by_sin[m], qk_hi[r][i], qk_lo[r][i]
                    if i == 0 and not isinstance(n, int):
                        pool.wait_ge(s_s[0], ONE + n * PAIRS - PAIRS)
                        pool.wait_ge(s_s[1], ONE + n * PAIRS - PAIRS)
                    pool.wait_ge(s_rope, ONE + 3 * (n * R + i + 1))
                    nc.gpsimd.tensor_tensor(hi[:], cos[:], sin[:], ALU.add).then_inc(s_rsum, 1)
                    nc.gpsimd.tensor_tensor(cos[:], cos[:], sin[:], ALU.add).then_inc(s_rsum, 1)
                    pool.wait_ge(s_rsum, ONE + 2 * (n * R + i + 1))
                    nc.gpsimd.tensor_tensor(lo[:], cos[:], hi[:], ALU.subtract).then_inc(s_rot, 1)

                for i in range(R):
                    rotate(0, i, 0)
                with pool.Fori(0, B * NKV // 2) as h:
                    for r in range(2):
                        for i in range(R):
                            rotate(2 * h + r + 1, i, 1 - r)

            @block.scalar
            def _(act):
                act.wait_ge(s_var, ONE + 1)
                nc.scalar.activation(work[:, 2, :], work[:, 2, :], ACT.Sqrt).then_inc(s_std, 1)
                for b in range(B):
                    act.wait_ge(s_xT, ONE + b + 1)
                    nc.scalar.activation(xT_hi[:, b * S:(b + 1) * S], psT[:], ACT.Copy).then_inc(s_xhi, 1)
                for k in range(-PROJ, LOOK):
                    act_take(act, 0, k)
                act_exp(act, 0, 0, 1)
                with act.Fori(0, B) as b:
                    for k in range(STEPS):
                        kind, a = SLOTS[k]
                        if kind == "pair":
                            act_probT(act, b, a, 0)
                            act_exp(act, b, a + 1, 1)
                            act_probT(act, b, a, 1)
                        act_take(act, b, k + LOOK)
                        if kind == "pair":
                            act_oT(act, b, a)


def build(nc, d, out):
    with ExitStack() as ctx:
        net = Net(nc, ctx)
        load_stage(net, d)
        attention_a(net)
        xn_dram = nc.dram_tensor("xn", (B * S, P), F32, kind="Internal").ap()
        acc_dram = [nc.dram_tensor(f"acc{i}", (B * S, P), F32, kind="Internal").ap() for i in range(2)]
        ffn(net, acc_dram[0], xn_dram)
        attention_b(net)
        ffn(net, acc_dram[1], xn_dram)
        with nc.Block() as block:
            s_out = net.sem(ctx, "out")

            @block.sync
            def _(sp):
                sp.dma_start(out.rearrange("(t p) c -> p t c", p=P), net.x[:]).then_inc(s_out, 16)
                sp.wait_ge(s_out, 16)


def kernel(**inputs):
    import ml_dtypes
    import numpy as np
    import concourse.bacc as bacc
    from concourse.bass_utils import run_bass_kernel_spmd

    a = {k: np.asarray(v) for k, v in inputs.items()}
    lay = np.ascontiguousarray
    wqkv = a["L0_attn_a_w_qkv"]
    arrays = {
        "x": lay(a["L0_attn_a_x"].reshape(B * S, P)),
        "wq_a": lay(wqkv[0:P]), "wk_a": lay(wqkv[P:2 * P]), "wv_aT": lay(wqkv[2 * P:].T),
        "wfc_T": lay(a["L0_attn_a_w_fc"].T),
        "bfc": lay(np.broadcast_to(a["L0_attn_a_b_fc"], (P, P))),
        "gamma": lay(np.broadcast_to(a["L0_attn_a_gamma"], (P, P))),
        "beta": lay(np.broadcast_to(a["L0_attn_a_beta"], (P, P))),
        "gate": a["L0_ffn_gate_w"],
        "wq": a["L0_attn_b_Wq"], "wk": a["L0_attn_b_Wk"], "wv": a["L0_attn_b_Wv"],
        "wo": lay(a["L0_attn_b_Wo"].reshape(NH, P, P).transpose(1, 0, 2).reshape(P, NH * P)),
        "w1": lay(a["L0_ffn_w1"].transpose(1, 0, 2).reshape(P, E * FC * P)),
        "w2": lay(a["L0_ffn_w2"].reshape(E, FC, P, P).transpose(2, 0, 1, 3).reshape(P, E * FC * P)),
    }
    half = np.arange(0, P, 2, dtype=np.float32) / np.float32(P)
    inv_freq = (np.float32(1.0) / np.power(np.float32(10000.0), half)).astype(np.float32)
    angle = np.outer(inv_freq, np.arange(S, dtype=np.float32)).astype(np.float32)
    arrays["cos"] = lay(np.concatenate([np.cos(angle)] * 2).astype(np.float32))
    arrays["sin"] = lay(np.concatenate([np.sin(angle), -np.sin(angle)]).astype(np.float32))
    arrays["ident"] = np.eye(P, dtype=np.float32)
    arrays["identb"] = np.eye(P, dtype=ml_dtypes.bfloat16)
    arrays["maskb"] = np.triu(np.full((P, P), -1e30, np.float32), 1).astype(ml_dtypes.bfloat16)
    arrays["rowbase"] = (np.arange(ROWS, dtype=np.float32) % B * S).reshape(ROWS, 1).astype(np.float32)
    nc = bacc.Bacc("TRN2", target_bir_lowering=False, num_devices=1)
    d = {k: nc.dram_tensor(f"in_{k}", v.shape, mybir.dt.from_np(v.dtype), kind="ExternalInput").ap()
         for k, v in arrays.items()}
    out = nc.dram_tensor("out", (B * S, P), F32, kind="ExternalOutput").ap()
    build(nc, d, out)
    r = run_bass_kernel_spmd(nc, [{f"in_{k}": v for k, v in arrays.items()}], core_ids=[0])
    return r.results[0]["out"].reshape(B, S, P)
```

```python
import concourse.bass as bass
from concourse import mybir
from contextlib import ExitStack

F32 = mybir.dt.float32
F16 = mybir.dt.float16
BF16 = mybir.dt.bfloat16
U32 = mybir.dt.uint32
ALU = mybir.AluOpType
ACT = mybir.ActivationFunctionType
AX_X = mybir.AxisListType.X

P = 128
B, S = 4, 1024
T = S // P
NT = B * T
NH, NKV = 8, 4
GROUP = NH // NKV
E = 8
FC = 4
CAP = 2 * S // E
CH = CAP // P
ROWS = E * B
SCALE = float(P) ** -0.5
EPS = 1e-5
ONE = 8
WS = 64.0


class Steps:

    def __init__(self, sem):
        self.sem, self.base, self.n, self.outer = sem, ONE, 0, []

    @property
    def at(self):
        return self.base + self.n

    def step(self, instruction, n=1):
        instruction.then_inc(self.sem, n)
        self.n += n
        return self.at

    def expect(self, n=1):
        self.n += n
        return self.at

    def enter(self, i, per):
        self.outer.append((self.base, self.n, per))
        self.base, self.n = self.base + self.n + i * per, 0

    def leave(self, rounds):
        base, n, per = self.outer.pop()
        assert self.n == per, (self.sem, self.n)
        self.base, self.n = base, n + rounds * per


def flat(ap):
    return ap.rearrange("p a b -> p (a b)")


class Net:

    def __init__(self, nc, ctx):
        self.nc, self.ctx = nc, ctx
        self.n = 0

    def sb(self, ctx, name, shape, dt=F32):
        self.n += 1
        return ctx.enter_context(self.nc.sbuf_tensor(f"{name}_{self.n}", shape, dt))

    def ps(self, ctx, name, shape, dt=F32):
        self.n += 1
        return ctx.enter_context(self.nc.psum_tensor(f"{name}_{self.n}", shape, dt))

    def sem(self, ctx, name):
        self.n += 1
        return ctx.enter_context(self.nc.semaphore(f"{name}_{self.n}"))

    def makers(self, ctx):
        self.stage_sems = []

        def sem(name, swdge=False):
            if swdge:
                return self.sem(ctx, name)
            self.stage_sems.append(self.sem(ctx, name))
            return self.stage_sems[-1]

        return (lambda *a: self.sb(ctx, *a)), (lambda *a: self.ps(ctx, *a)), sem

    def raise_sems(self):
        with self.nc.Block() as block:
            @block.sync
            def _(sp):
                for s in self.stage_sems:
                    sp.sem_inc(s, ONE)


def load_stage(net, d, first):
    nc, ctx = net.nc, net.ctx
    net.x = net.sb(ctx, "x", [P, NT, P])
    net.stats = net.sb(ctx, "x_stats", [P, NT, 6])
    early = {"wq_a": P, "wk_a": P, "wv_aT": P, "wfc_T": P, "bfc": P, "gamma": P, "beta": P}
    plain = {"gate": E,
             "wo": NH * P, "cos": S, "sin": S, "ident": P, "identb": P, "maskb": P, "iota": S,
             "rowbase": CH * ROWS, "number": T, "ones": P, "upto": P}
    types = {"identb": BF16, "maskb": BF16, "iota": F16, "ones": F16, "upto": F16}
    net.w = {k: net.sb(ctx, k, [P, n], types.get(k, F32)) for k, n in plain.items()}
    parts = {"w1": E * FC * P, "w2": E * FC * P, "wq": NH * P, "wk": NKV * P, "wv": NKV * P}
    net.hi = {k: net.sb(ctx, k + "_hi", [P, n], F16) for k, n in parts.items()}
    net.lo = {k: net.sb(ctx, k + "_lo", [P, n], F16) for k, n in parts.items()}
    net.w.update({k: net.sb(first, k, [P, n]) for k, n in early.items()})
    net.raw = {k: net.sb(first, k + "_raw", [P, n]) for k, n in parts.items()}
    net.s_raw = {k: net.sem(first, k + "_loaded") for k in parts}
    s_rest = net.sem(first, "rest_loaded")
    s_x = [net.sem(first, f"x_loaded{b}") for b in range(B)]
    with nc.Block() as block:
        @block.sync
        def _(sp):
            x_tiles = d["x"].rearrange("(t p) c -> p t c", p=P)
            n = 0
            for b in range(B):
                sp.dma_start(net.x[:, b * T:(b + 1) * T, :], x_tiles[:, b * T:(b + 1) * T, :]).then_inc(s_x[b], 16)
            for k in (*early, *plain):
                sp.dma_start(net.w[k][:], d[k]).then_inc(s_rest, 16)
                n += 16
            for k in parts:
                sp.dma_start(net.raw[k][:], d[k]).then_inc(net.s_raw[k], 16)
            sp.wait_ge(s_rest, n)

        @block.vector
        def _(dve):
            for b in range(B):
                dve.wait_ge(s_x[b], 16)
                tile_stats(net, b, range(T))


def norm_var(nc, dve, done, sem_var, stats, work, mean):
    me, mo, ve, vo = stats[:, :, 1], stats[:, :, 4], stats[:, :, 2], stats[:, :, 5]
    total, diff, var, sq = work[:, 0, :], work[:, 1, :], work[:, 2, :], work[:, 3, :]
    done.step(nc.vector.tensor_tensor(total, me, mo, ALU.add))
    done.step(nc.vector.tensor_tensor(diff, me, mo, ALU.subtract))
    done.step(nc.vector.tensor_tensor(var, ve, vo, ALU.add))
    dve.wait_ge(done.sem, done.at)
    done.step(nc.vector.tensor_scalar(mean, total, 0.5, None, op0=ALU.mult))
    done.step(nc.vector.tensor_tensor(sq, diff, diff, ALU.mult))
    dve.wait_ge(done.sem, done.at)
    done.step(nc.vector.tensor_scalar(sq, sq, 0.25, EPS, op0=ALU.mult, op1=ALU.add))
    dve.wait_ge(done.sem, done.at)
    sem_var.step(nc.vector.scalar_tensor_tensor(var, var, 1.0 / P, sq, ALU.mult, ALU.add))


def norm_stats(nc, dve, done, sem_var, sem_std, stats, work, mean, rstd):
    norm_var(nc, dve, done, sem_var, stats, work, mean)
    dve.wait_ge(sem_std.sem, sem_std.expect())
    done.step(nc.vector.reciprocal(rstd, work[:, 2, :]))
    dve.wait_ge(done.sem, done.at)


def tile_stats(net, b, tiles):
    for t in tiles:
        i = bass.ds(b * T + t, 1)
        net.nc.vector.bn_stats(net.stats[:, i, :].rearrange("p a b -> p (a b)"),
                               net.x[:, i, :].rearrange("p a b -> p (a b)"))


def attention_a(net):
    nc, w = net.nc, net.w
    with ExitStack() as ctx:
        sb, ps, sem = net.makers(ctx)
        work = sb("work", [P, 4, NT])
        mean, rstd = sb("mean", [P, NT]), sb("rstd", [P, NT])
        xs = [sb(f"xs{i}", [P, T, P]) for i in range(2)]
        xT_hi, xT_lo, qg_hi, qg_lo = ([sb(f"{n}{i}", [P, S], F16) for i in range(2)]
                                      for n in ("xT_hi", "xT_lo", "qg_hi", "qg_lo"))
        crow = [sb(f"crow{i}", [P, P]) for i in range(2)]
        nmax, nbias, rowsum = (sb(n, [P, 2, T]) for n in ("nmax", "nbias", "rowsum"))
        g_hi, g_lo = sb("g_hi", [P, P], F16), sb("g_lo", [P, P], F16)
        xsum, vsum, vsum_b = sb("xsum", [P, 1]), sb("vsum", [P, 1]), sb("vsum_b", [P, P])
        prob = sb("prob", [P, 2, S])
        rinv, wsum = sb("rinv", [P, T]), sb("wsum", [P, T])
        h = sb("h", [P, T, P])
        hn = sb("hn", [P, T, P])
        hstats, hwork = sb("hstats", [P, T, 6]), sb("hwork", [P, 4, T])
        hmean, hrstd = sb("hmean", [P, T]), sb("hrstd", [P, T])
        psT = ps("psT", [P, S])
        psS = [ps(f"psS{i}", [P, S]) for i in range(2)]
        psC = ps("psC", [P, 512])

        s_var, s_std = sem("var"), sem("std")
        s_dve, s_pool = sem("dve"), sem("pool")
        chunks = [(k, slice(c, min(c + S, raw.shape[1]))) for k, raw in net.raw.items() for c in range(0, raw.shape[1], S)]
        s_high, s_scaled, s_pool_scaled = sem("weights_high"), sem("weights_scaled"), sem("pool_scaled")
        s_g, s_ghi, s_glo = sem("g"), sem("g_hi"), sem("g_lo")
        s_xs, s_xT, s_xhi, s_xlo = sem("xs"), sem("xT"), sem("x_hi"), sem("x_lo")
        s_qg, s_qghi, s_qglo = sem("qg"), sem("qg_hi"), sem("qg_lo")
        s_xsum, s_v, s_vb, s_c = sem("xsum"), sem("v"), sem("v_b"), sem("c")
        s_s, s_nb, s_exp, s_hn, s_hvar, s_hstd = sem("scores"), sem("nbias"), sem("exp"), sem("hn"), sem("hvar"), sem("hstd")

        net.raise_sems()
        with nc.Block() as block:
            @block.tensor
            def _(pe):
                pe.matmul(psC[:, 0:P], w["wq_a"][:], w["wk_a"][:], start=True, stop=True).then_inc(s_g, 1)

                def turn(b):
                    pe.wait_ge(s_xs, ONE + (b + 1) * T)
                    if b:
                        pe.wait_ge(s_qglo, ONE + b)
                    for t in range(T):
                        last = pe.transpose(psT[:, t * P:(t + 1) * P], xs[b % 2][:, t, :], w["ident"][:])
                    last.then_inc(s_xT, 1)

                def through_wv(b):
                    pe.wait_ge(s_xsum, ONE + b + 1)
                    pe.matmul(psC[:, P:P + 1], w["wv_aT"][:], xsum[:], start=True, stop=True).then_inc(s_v, 1)

                def through_wfc(b):
                    pe.wait_ge(s_vb, ONE + b + 1)
                    pe.matmul(psC[:, 2 * P:3 * P], vsum_b[:], w["wfc_T"][:], start=True, stop=True).then_inc(s_c, 1)

                def queries(b):
                    pe.wait_ge(s_xlo, ONE + b + 1)
                    if b == 0:
                        pe.wait_ge(s_glo, ONE + 1)
                    hi, lo = xT_hi[b % 2], xT_lo[b % 2]
                    for c in range(2):
                        cols = slice(c * 512, (c + 1) * 512)
                        for i, (l, r) in enumerate(((g_hi, hi), (g_hi, lo), (g_lo, hi))):
                            last = pe.matmul(psT[:, cols], l[:], r[:, cols], start=(i == 0), stop=(i == 2))
                    last.then_inc(s_qg, 1)

                def scores(b, t):
                    if t == 0:
                        pe.wait_ge(s_qglo, ONE + b + 1)
                    if b * T + t >= 2:
                        pe.wait_ge(s_exp, ONE + b * T + t - 1)
                    r = b % 2
                    for c in range(2):
                        cols = slice(c * 512, (c + 1) * 512)
                        for i, (l, k) in enumerate(((qg_hi, xT_hi), (qg_hi, xT_lo), (qg_lo, xT_hi))):
                            last = pe.matmul(psS[t % 2][:, cols], l[r][:, t * P:(t + 1) * P], k[r][:, cols],
                                             start=(i == 0), stop=(i == 2))
                    last.then_inc(s_s, 1)

                ahead = {3: (turn,), 5: (through_wv,), 6: (through_wfc, queries)}
                for step in (turn, through_wv, through_wfc, queries):
                    step(0)
                for b in range(B):
                    for t in range(T):
                        scores(b, t)
                        if b + 1 < B:
                            for step in ahead.get(t, ()):
                                step(b + 1)

            @block.vector
            def _(dve):
                done, var, std = Steps(s_dve), Steps(s_var), Steps(s_std)
                hvar, hstd = Steps(s_hvar), Steps(s_hstd)

                def settle():
                    dve.wait_ge(done.sem, done.at)

                def norm_x(b):
                    if b >= 2:
                        dve.wait_ge(s_xT, ONE + b - 1)
                    for t in range(T):
                        i = b * T + t
                        nc.vector.tensor_scalar(xs[b % 2][:, t, :], net.x[:, i, :], mean[:, i:i + 1], rstd[:, i:i + 1],
                                                op0=ALU.subtract, op1=ALU.mult).then_inc(s_xs, 1)

                def sum_x(b):
                    dve.wait_ge(s_xT, ONE + b + 1)
                    if b:
                        dve.wait_ge(s_v, ONE + b)
                    nc.vector.reduce_sum(xsum[:], psT[:], AX_X).then_inc(s_xsum, 1)

                def xT_low(b):
                    dve.wait_ge(s_xhi, ONE + b + 1)
                    nc.vector.tensor_tensor(xT_lo[b % 2][:], psT[:], xT_hi[b % 2][:], ALU.subtract).then_inc(s_xlo, 1)

                def spread_v(b):
                    dve.wait_ge(s_v, ONE + b + 1)
                    if b:
                        dve.wait_ge(s_c, ONE + b)
                    done.step(nc.vector.tensor_copy(vsum[:], psC[:, P:P + 1]))
                    settle()
                    nc.vector.tensor_copy(vsum_b[:], vsum[:].to_broadcast([P, P])).then_inc(s_vb, 1)

                def take_c(b):
                    dve.wait_ge(s_c, ONE + b + 1)
                    done.step(nc.vector.tensor_copy(crow[b % 2][:], psC[:, 2 * P:3 * P]))

                def queries_low(b):
                    dve.wait_ge(s_qghi, ONE + b + 1)
                    nc.vector.tensor_tensor(qg_lo[b % 2][:], psT[:], qg_hi[b % 2][:], ALU.subtract).then_inc(s_qglo, 1)

                def row_max(b, t):
                    r = b % 2
                    dve.wait_ge(s_s, ONE + b * T + t + 1)
                    done.step(nc.vector.reduce_max(nmax[:, r, t:t + 1], psS[t % 2][:], AX_X, negate=True))
                    settle()
                    nc.vector.tensor_scalar(nbias[:, r, t:t + 1], nmax[:, r, t:t + 1], SCALE / WS, None,
                                            op0=ALU.mult).then_inc(s_nb, 1)

                def add_rows(b):
                    dve.wait_ge(s_exp, ONE + (b + 1) * T)
                    done.step(nc.vector.reciprocal(rinv[:], rowsum[:, b % 2]))
                    settle()
                    done.step(nc.vector.tensor_tensor(wsum[:], rinv[:], rowsum[:, b % 2], ALU.mult))
                    settle()
                    for t in range(T):
                        done.step(nc.vector.scalar_tensor_tensor(h[:, t, :], crow[b % 2][:], wsum[:, t:t + 1],
                                                                 xs[b % 2][:, t, :], ALU.mult, ALU.add))
                    settle()

                def add_bias(b):
                    done.step(nc.vector.tensor_tensor(h[:], h[:], w["bfc"][:, None, :].to_broadcast([P, T, P]), ALU.add))
                    settle()
                    for t in range(T):
                        done.step(nc.vector.bn_stats(hstats[:, t, :], h[:, t, :]))
                    settle()

                def rows_var(b):
                    norm_var(nc, dve, done, hvar, hstats, hwork, hmean[:])

                def norm_rows(b):
                    dve.wait_ge(s_hstd, hstd.expect())
                    done.step(nc.vector.reciprocal(hrstd[:], hwork[:, 2, :]))
                    settle()
                    if b:
                        dve.wait_ge(s_pool, ONE + 3 * b)
                    for t in range(T):
                        nc.vector.tensor_scalar(hn[:, t, :], h[:, t, :], hmean[:, t:t + 1], hrstd[:, t:t + 1],
                                                op0=ALU.subtract, op1=ALU.mult).then_inc(s_hn, 1)

                def stats_of_new(b):
                    dve.wait_ge(s_pool, ONE + 3 * b + 3)
                    tile_stats(net, b, range(T))

                dve.wait_ge(s_ghi, ONE + 1)
                nc.vector.scalar_tensor_tensor(g_lo[:], psC[:, 0:P], WS, g_hi[:], ALU.mult, ALU.subtract).then_inc(s_glo, 1)
                norm_stats(nc, dve, done, var, std, net.stats, work, mean[:], rstd[:])
                for step in (norm_x, sum_x, xT_low, spread_v, take_c, queries_low):
                    step(0)
                behind = {0: (add_rows,), 1: (add_bias,), 2: (rows_var,), 4: (norm_rows,), 7: (stats_of_new,)}
                ahead = {0: (norm_x,), 3: (sum_x,), 4: (xT_low,), 5: (spread_v,), 6: (take_c,), 7: (queries_low,)}
                for b in range(B):
                    for t in range(T):
                        row_max(b, t)
                        if b:
                            for step in behind.get(t, ()):
                                step(b - 1)
                        if b + 1 < B:
                            for step in ahead.get(t, ()):
                                step(b + 1)
                for step in (add_rows, add_bias, rows_var, norm_rows):
                    step(B - 1)
                dve.wait_ge(s_hn, ONE + B * T)
                rows = net.x[:, (B - 1) * T:, :]
                done.step(nc.vector.tensor_tensor(hn[:], hn[:], w["gamma"][:, None, :].to_broadcast([P, T, P]), ALU.mult))
                settle()
                done.step(nc.vector.tensor_tensor(hn[:], hn[:], w["beta"][:, None, :].to_broadcast([P, T, P]), ALU.add))
                settle()
                done.step(nc.vector.tensor_tensor(rows, rows, hn[:], ALU.add))
                settle()
                tile_stats(net, B - 1, range(T))

            @block.scalar
            def _(act):
                act.wait_ge(s_g, ONE + 1)
                nc.scalar.activation(g_hi[:], psC[:, 0:P], ACT.Copy, scale=WS).then_inc(s_ghi, 1)
                act.wait_ge(s_var, ONE + 1)
                nc.scalar.activation(work[:, 2, :], work[:, 2, :], ACT.Sqrt).then_inc(s_std, 1)

                def xT_high(b):
                    act.wait_ge(s_xsum, ONE + b + 1)
                    if b >= 2:
                        act.wait_ge(s_s, ONE + (b - 1) * T)
                    nc.scalar.activation(xT_hi[b % 2][:], psT[:], ACT.Copy).then_inc(s_xhi, 1)

                def queries_high(b):
                    act.wait_ge(s_qg, ONE + b + 1)
                    nc.scalar.activation(qg_hi[b % 2][:], psT[:], ACT.Copy).then_inc(s_qghi, 1)

                def root(b):
                    act.wait_ge(s_hvar, ONE + b + 1)
                    nc.scalar.activation(hwork[:, 2, :], hwork[:, 2, :], ACT.Sqrt).then_inc(s_hstd, 1)

                xT_high(0)
                queries_high(0)

                def weights(n):
                    k, cols = chunks[n]
                    if cols.start == 0:
                        act.wait_ge(net.s_raw[k], 16)
                    raw = net.raw[k][:, cols]
                    nc.scalar.activation(net.hi[k][:, cols], raw, ACT.Copy, scale=WS).then_inc(s_high, 1)
                    if n % 2 == 0:
                        act.wait_ge(s_high, ONE + n + 1)
                        nc.scalar.activation(raw, raw, ACT.Copy, scale=WS).then_inc(s_scaled, 1)

                ahead = {3: (xT_high,), 6: (queries_high,)}
                for b in range(B):
                    for t in range(T):
                        n = b * T + t
                        act.wait_ge(s_nb, ONE + n + 1)
                        if n >= 2:
                            act.wait_ge(s_exp, ONE + n - 1)
                        nc.scalar.activation(prob[:, t % 2, :], psS[t % 2][:], ACT.Exp, bias=nbias[:, b % 2, t:t + 1],
                                             scale=SCALE / WS, accum_out=rowsum[:, b % 2, t:t + 1]).then_inc(s_exp, 1)
                        if b and t == 2:
                            root(b - 1)
                        if n < len(chunks):
                            weights(n)
                        if b + 1 < B:
                            for step in ahead.get(t, ()):
                                step(b + 1)
                root(B - 1)

            @block.gpsimd
            def _(pool):
                for n, (k, cols) in enumerate(chunks):
                    if n % 2:
                        pool.wait_ge(s_high, ONE + n + 1)
                        nc.gpsimd.tensor_scalar(net.raw[k][:, cols], net.raw[k][:, cols], WS, None, op0=ALU.mult
                                                ).then_inc(s_pool_scaled, 1)
                        pool.wait_ge(s_pool_scaled, ONE + n // 2 + 1)
                    else:
                        pool.wait_ge(s_scaled, ONE + n // 2 + 1)
                    nc.gpsimd.tensor_tensor(net.lo[k][:, cols], net.raw[k][:, cols], net.hi[k][:, cols], ALU.subtract)
                with pool.Fori(0, B - 1) as b:
                    rows = net.x[:, bass.ds(b * T, T), :]
                    pool.wait_ge(s_hn, ONE + (b + 1) * T)
                    nc.gpsimd.tensor_tensor(hn[:], hn[:], w["gamma"][:, None, :].to_broadcast([P, T, P]), ALU.mult).then_inc(s_pool, 1)
                    pool.wait_ge(s_pool, ONE + b * 3 + 1)
                    nc.gpsimd.tensor_tensor(hn[:], hn[:], w["beta"][:, None, :].to_broadcast([P, T, P]), ALU.add).then_inc(s_pool, 1)
                    pool.wait_ge(s_pool, ONE + b * 3 + 2)
                    nc.gpsimd.tensor_tensor(rows, rows, hn[:], ALU.add).then_inc(s_pool, 1)


def ffn(net, xn_dram, out=None):
    with ExitStack() as ctx:
        idx = net.sb(ctx, "idx", [P, CH, ROWS], U32)
        token = net.sb(ctx, "token", [P, CH, ROWS])
        weight = net.sb(ctx, "weight", [P, CH, ROWS])
        ffn_route(net, xn_dram, idx, token, weight)
        ffn_experts(net, xn_dram, idx, token, weight, out)


def ffn_route(net, xn_dram, idx, token, weight):
    nc, w = net.nc, net.w
    PARTS = 3
    UP = 2.0 ** 15
    COLS = 1 + PARTS
    FINE = 32
    COARSE = CAP // FINE
    QUARTERS = P // FINE
    GROUPS = ROWS // QUARTERS
    TRIES = 3
    FACTORS = ((32, 64, 96), (8, 16, 24), (2, 4, 6))
    ROUND = 1.5 * 2.0 ** 23
    LEAST = 2.0 ** -126
    MANTISSA = 23
    FINER = (MANTISSA - 1) // 2
    with ExitStack() as ctx:
        sb, ps, sem = net.makers(ctx)
        work = sb("work", [P, 4, NT])
        mean, rstd = sb("mean", [P, NT]), sb("rstd", [P, NT])
        xs = [sb(f"xs{i}", [P, T, P]) for i in range(2)]
        xT_hi, xT_lo = ([sb(f"xT_{n}{i}", [P, S], F16) for i in range(2)] for n in ("hi", "lo"))
        gate_hi, gate_lo = sb("gate_hi", [P, E], F16), sb("gate_lo", [P, E], F16)
        logits, prob = sb("logits", [P, NT, E]), sb("prob", [P, NT, E])
        pairs = sb("pairs", [P, T, ROWS])
        top, tot = sb("top", [P, NT]), sb("tot", [P, NT])
        reach, base, unit, twice = (sb(n, [P, ROWS]) for n in ("reach", "base", "unit", "twice"))
        tries, adds, found = sb("tries", [P, TRIES, ROWS]), sb("adds", [P, TRIES, ROWS]), sb("found", [P, 1 + TRIES, ROWS])
        reached = sb("reached", [P, TRIES, T, ROWS], F16)
        above, equal, taken = (sb(n, [P, T, ROWS], F16) for n in ("above", "equal", "taken"))
        room, slot, part = sb("room", [P, ROWS]), sb("slot", [P, T, ROWS]), sb("part", [P, T, ROWS])
        whole = sb("whole", [P, T, ROWS])
        coarse, fine = sb("coarse", [P, T, ROWS], F16), sb("fine", [P, T, ROWS], F16)
        cols = sb("cols", [P, B, T * E, COLS], F16)
        is_coarse, is_fine = sb("is_coarse", [P, B, T * E, COARSE], F16), sb("is_fine", [P, B, T * E, FINE], F16)
        moved = sb("moved", [P, B, T * E, COLS, COARSE], F16)
        summed = sb("summed", [P, GROUPS, QUARTERS, COARSE])
        psT = [ps(f"psT{i}", [P, S]) for i in range(2)]
        psL = ps("psL", [P, 512])
        psC = ps("psC", [P, 512])
        psR = ps("psR", [P, 512])
        lists = psT[0][:].rearrange("p (g q k c) -> p g q k c", g=GROUPS, q=QUARTERS, k=COLS)
        s_var, s_std, s_dve = sem("var"), sem("std"), sem("dve")
        s_xs, s_xT, s_xhi, s_xlo, s_lg, s_gate = sem("xs"), sem("xT"), sem("x_hi"), sem("x_lo"), sem("logits"), sem("gate")
        s_xn = [sem(f"xn_dram{i}") for i in range(2)]
        s_sub, s_exp, s_mask, s_count = sem("sub"), sem("exp"), sem("mask"), sem("count")
        s_rank, s_fine, s_moved, s_listed = sem("rank"), sem("is_fine"), sem("moved"), sem("listed")
        s_numbers = sem("numbers_moved")
        s_coarse, s_cols, s_pairs, s_pool = sem("is_coarse"), sem("cols"), sem("pairs"), sem("pool")
        xn_tiles = xn_dram.rearrange("(t p) c -> p t c", p=P)
        ROUNDS = len(FACTORS) + 1 + FINER
        assert 2 * FINER == MANTISSA - 1

        def by_sequence(te):
            return te.rearrange("p b (t e) -> p t b e", t=T)

        def rows_of(tr):
            return tr.rearrange("p t (b e) -> p t b e", b=B)

        def move(engine, b, k):
            return engine.tensor_tensor(moved[:, b, :, k, :], is_coarse[:, b],
                                        cols[:, b, :, k][:, :, None].to_broadcast([P, T * E, COARSE]), ALU.mult)

        def over_tiles(rows):
            return rows[:, None, :].to_broadcast([P, T, ROWS])

        net.raise_sems()
        with nc.Block() as block:
            @block.sync
            def _(sp):
                for b in range(B):
                    sp.wait_ge(s_xs, ONE + (b + 1) * T)
                    sp.dma_start(xn_tiles[:, b * T:(b + 1) * T, :], xs[b % 2][:]).then_inc(s_xn[b % 2], 16)
                for i in range(2):
                    sp.wait_ge(s_xn[i], ONE + 16 * B // 2)

            @block.tensor
            def _(pe):
                def turn(b):
                    pe.wait_ge(s_xs, ONE + (b + 1) * T)
                    if b >= 2:
                        pe.wait_ge(s_xlo, ONE + b - 1)
                    for t in range(T):
                        last = pe.transpose(psT[b % 2][:, t * P:(t + 1) * P], xs[b % 2][:, t, :], w["ident"][:])
                    last.then_inc(s_xT, 1)

                turn(0)
                for b in range(B):
                    if b + 1 < B:
                        turn(b + 1)
                    pe.wait_ge(s_xlo, ONE + b + 1)
                    if b == 0:
                        pe.wait_ge(s_gate, ONE + 2)
                    for t in range(T):
                        at = (b * T + t) * E
                        for i, (l, r) in enumerate(((xT_hi, gate_hi), (xT_hi, gate_lo), (xT_lo, gate_hi))):
                            last = pe.matmul(psL[:, at:at + E], l[b % 2][:, t * P:(t + 1) * P], r[:],
                                             start=(i == 0), stop=(i == 2))
                    last.then_inc(s_lg, 1)

                def count(mask, k=0):
                    for t in range(T):
                        last = pe.matmul(psC[:, k * ROWS:(k + 1) * ROWS], w["ones"][:], mask[:, t, :],
                                         start=(t == 0), stop=(t == T - 1))
                    last.then_inc(s_count, 1)

                def rank(mask):
                    for t in range(T):
                        for i in range(t + 1):
                            last = pe.matmul(psR[:, t * ROWS:(t + 1) * ROWS], w["upto" if i == t else "ones"][:],
                                             mask[:, i, :], start=(i == 0), stop=(i == t))
                    last.then_inc(s_rank, 1)

                with pe.Fori(0, ROUNDS) as n:
                    for k in range(TRIES):
                        pe.wait_ge(s_mask, ONE + TRIES * n + k + 1)
                        count(reached[:, k], k)
                for i in range(2):
                    pe.wait_ge(s_mask, ONE + TRIES * ROUNDS + i + 1)
                    count(above)
                pe.wait_ge(s_mask, ONE + TRIES * ROUNDS + 3)
                rank(equal)
                pe.wait_ge(s_mask, ONE + TRIES * ROUNDS + 4)
                rank(taken)
                with pe.Fori(0, B) as b:
                    pe.wait_ge(s_fine, ONE + b + 1)
                    pe.wait_ge(s_numbers, ONE + b + 1)
                    pe.wait_ge(s_moved, ONE + PARTS * (b + 1))
                    for g in range(E // QUARTERS):
                        for t in range(T):
                            rows = slice(t * E + g * QUARTERS, t * E + (g + 1) * QUARTERS)
                            group = bass.ds(b * (E // QUARTERS) + g, 1)
                            last = pe.matmul(lists[:, group].rearrange("p a q k c -> p (a q k c)"),
                                             is_fine[:, bass.ds(b, 1), rows, :].rearrange("p a r f -> p (a r f)"),
                                             moved[:, bass.ds(b, 1), rows].rearrange("p a r k c -> p (a r k c)"),
                                             start=(t == 0), stop=(t == T - 1))
                    last.then_inc(s_listed, 1)

            @block.gpsimd
            def _(pool):
                pool.wait_ge(s_pairs, ONE + 1)
                nc.gpsimd.tensor_copy(by_sequence(cols[:, :, :, 0]), w["number"][:][:, :, None, None].to_broadcast([P, T, B, E])
                                      ).then_inc(s_cols, 1)
                nc.gpsimd.tensor_scalar(part[:], pairs[:], UP, None, op0=ALU.mult).then_inc(s_pool, 1)
                for k in range(PARTS):
                    pool.wait_ge(s_pool, ONE + 1 + k)
                    nc.gpsimd.tensor_copy(by_sequence(cols[:, :, :, 1 + k]), rows_of(part[:])).then_inc(s_cols, 1)
                    if k < PARTS - 1:
                        pool.wait_ge(s_cols, ONE + 2 + k)
                        nc.gpsimd.tensor_tensor(rows_of(part[:]), rows_of(part[:]), by_sequence(cols[:, :, :, 1 + k]),
                                                ALU.subtract).then_inc(s_pool, 1)
                pool.wait_ge(s_cols, ONE + COLS)
                for b in range(B):
                    pool.wait_ge(s_coarse, ONE + b + 1)
                    for k in range(1, COLS):
                        move(nc.gpsimd, b, k).then_inc(s_moved, 1)

            @block.scalar
            def _(act):
                act.wait_ge(s_var, ONE + 1)
                nc.scalar.activation(work[:, 2, :], work[:, 2, :], ACT.Sqrt).then_inc(s_std, 1)
                for b in range(B):
                    act.wait_ge(s_xT, ONE + b + 1)
                    if b >= 2:
                        act.wait_ge(s_lg, ONE + b - 1)
                    nc.scalar.activation(xT_hi[b % 2][:], psT[b % 2][:], ACT.Copy).then_inc(s_xhi, 1)
                act.wait_ge(s_sub, ONE + 1)
                nc.scalar.activation(prob[:], prob[:], ACT.Exp).then_inc(s_exp, 1)

            @block.vector
            def _(dve):
                done, var, std, mask = Steps(s_dve), Steps(s_var), Steps(s_std), Steps(s_mask)
                counts = Steps(s_count)

                def settle():
                    dve.wait_ge(done.sem, done.at)

                norm_stats(nc, dve, done, var, std, net.stats, work, mean[:], rstd[:])

                def norm_x(b):
                    if b >= 2:
                        dve.wait_ge(s_xT, ONE + b - 1)
                        dve.wait_ge(s_xn[b % 2], ONE + 16 * (b // 2))
                    for t in range(T):
                        i = b * T + t
                        nc.vector.tensor_scalar(xs[b % 2][:, t, :], net.x[:, i, :], mean[:, i:i + 1], rstd[:, i:i + 1],
                                                op0=ALU.subtract, op1=ALU.mult).then_inc(s_xs, 1)

                def xT_low(b):
                    dve.wait_ge(s_xhi, ONE + b + 1)
                    nc.vector.tensor_tensor(xT_lo[b % 2][:], psT[b % 2][:], xT_hi[b % 2][:], ALU.subtract).then_inc(s_xlo, 1)

                norm_x(0)
                nc.vector.tensor_scalar(gate_hi[:], w["gate"][:], WS, None, op0=ALU.mult).then_inc(s_gate, 1)
                dve.wait_ge(s_gate, ONE + 1)
                nc.vector.scalar_tensor_tensor(gate_lo[:], w["gate"][:], WS, gate_hi[:], ALU.mult,
                                               ALU.subtract).then_inc(s_gate, 1)
                norm_x(1)
                for b in range(B):
                    xT_low(b)
                    if b + 2 < B:
                        norm_x(b + 2)
                dve.wait_ge(s_lg, ONE + B)
                done.step(nc.vector.tensor_scalar(logits[:].rearrange("p n e -> p (n e)"), psL[:, 0:NT * E], 1.0 / WS, None,
                                                  op0=ALU.mult))
                settle()
                done.step(nc.vector.reduce_max(top[:], logits[:], AX_X))
                settle()
                nc.vector.tensor_tensor(prob[:], logits[:], top[:][:, :, None].to_broadcast([P, NT, E]),
                                        ALU.subtract).then_inc(s_sub, 1)
                done.step(nc.vector.memset(reach[:], LEAST))
                dve.wait_ge(s_exp, ONE + 1)
                done.step(nc.vector.reduce_sum(tot[:], prob[:], AX_X))
                settle()
                done.step(nc.vector.reciprocal(tot[:], tot[:]))
                settle()
                for b in range(B):
                    rows = slice(b * T, (b + 1) * T)
                    done.step(nc.vector.tensor_tensor(pairs[:, :, b * E:(b + 1) * E], prob[:, rows, :],
                                                      tot[:, rows][:, :, None].to_broadcast([P, T, E]), ALU.mult))
                settle()
                dve.sem_inc(s_pairs, 1)

                def probe(meanwhile=None):
                    for k in range(TRIES):
                        mask.step(nc.vector.tensor_tensor(reached[:, k], pairs[:], over_tiles(tries[:, k, :]), ALU.is_ge))
                    done.step(nc.vector.tensor_copy(found[:, 0, :], reach[:]))
                    if meanwhile is not None:
                        meanwhile()
                    dve.wait_ge(s_count, counts.expect(TRIES))
                    done.step(nc.vector.scalar_tensor_tensor(
                        found[:, 1:, :], psC[:, 0:TRIES * ROWS].rearrange("p (k r) -> p k r", k=TRIES), float(CAP), tries[:],
                        ALU.is_ge, ALU.mult))
                    settle()
                    done.step(nc.vector.reduce_max(reach[:], found[:].rearrange("p k r -> p r k"), AX_X))
                    settle()

                def times(factors):
                    for i, factor in enumerate(factors):
                        done.step(nc.vector.tensor_scalar(tries[:, i, :], reach[:], factor, None, op0=ALU.mult))
                    settle()

                for powers in FACTORS:
                    times([2.0 ** p for p in powers])
                    probe()
                done.step(nc.vector.tensor_copy(base[:], reach[:]))
                times((1.5, 2.0, 3.0))
                probe()
                done.step(nc.vector.scalar_tensor_tensor(twice[:], base[:], 2.0, reach[:], ALU.mult, ALU.is_le))
                settle()
                done.step(nc.vector.scalar_tensor_tensor(unit[:], twice[:], 1.0, base[:], ALU.add, ALU.mult))
                settle()
                for i in range(TRIES):
                    done.step(nc.vector.tensor_scalar(adds[:, i, :], unit[:], (i + 1) / 8, None, op0=ALU.mult))
                settle()

                def next_bits():
                    done.step(nc.vector.tensor_scalar(adds[:], adds[:], 0.25, None, op0=ALU.mult))

                for _ in range(FINER):
                    done.step(nc.vector.tensor_tensor(tries[:], reach[:][:, None, :].to_broadcast([P, TRIES, ROWS]), adds[:],
                                                      ALU.add))
                    settle()
                    probe(next_bits)
                mask.step(nc.vector.tensor_tensor(above[:], pairs[:], over_tiles(reach[:]), ALU.is_ge))
                dve.wait_ge(s_count, counts.expect())
                done.step(nc.vector.scalar_tensor_tensor(reach[:], psC[:, 0:ROWS], float(CAP), reach[:],
                                                         ALU.is_ge, ALU.mult))
                settle()
                mask.step(nc.vector.tensor_tensor(above[:], pairs[:], over_tiles(reach[:]), ALU.is_gt))
                mask.step(nc.vector.tensor_tensor(equal[:], pairs[:], over_tiles(reach[:]), ALU.is_equal))
                dve.wait_ge(s_count, counts.expect())
                done.step(nc.vector.tensor_scalar(room[:], psC[:, 0:ROWS], -1.0, float(CAP), op0=ALU.mult, op1=ALU.add))
                settle()
                dve.wait_ge(s_rank, ONE + 1)
                ranks = psR[:, 0:T * ROWS].rearrange("p (t r) -> p t r", t=T)
                done.step(nc.vector.tensor_tensor(slot[:], ranks, over_tiles(room[:]), ALU.is_le))
                settle()
                done.step(nc.vector.tensor_tensor(equal[:], slot[:], equal[:], ALU.mult))
                settle()
                mask.step(nc.vector.tensor_tensor(taken[:], above[:], equal[:], ALU.add))
                dve.wait_ge(s_mask, mask.at)
                dve.wait_ge(s_rank, ONE + 2)
                done.step(nc.vector.tensor_tensor(slot[:], ranks, taken[:], ALU.mult))
                settle()
                done.step(nc.vector.tensor_scalar(slot[:], slot[:], -1.0, None, op0=ALU.add))
                settle()
                done.step(nc.vector.tensor_scalar(whole[:], slot[:], 1.0 / FINE, -0.5 + 0.5 / FINE, op0=ALU.mult, op1=ALU.add))
                settle()
                done.step(nc.vector.tensor_scalar(whole[:], whole[:], ROUND, None, op0=ALU.add))
                settle()
                done.step(nc.vector.tensor_scalar(whole[:], whole[:], -ROUND, None, op0=ALU.add))
                settle()
                done.step(nc.vector.tensor_copy(coarse[:], whole[:]))
                done.step(nc.vector.scalar_tensor_tensor(fine[:], whole[:], -float(FINE), slot[:], ALU.mult, ALU.add))
                settle()

                def where(out, part, b):
                    n = out.shape[3]
                    return nc.vector.tensor_tensor(out[:, b].rearrange("p (t e) n -> p t e n", t=T),
                                                   w["iota"][:, 0:n][:, None, None, :].to_broadcast([P, T, E, n]),
                                                   part[:, :, b * E:(b + 1) * E][:, :, :, None].to_broadcast([P, T, E, n]),
                                                   ALU.is_equal)

                dve.wait_ge(s_cols, ONE + 1)
                where(is_coarse, coarse, 0).then_inc(s_coarse, 1)
                for b in range(B):
                    where(is_fine, fine, b).then_inc(s_fine, 1)
                    if b + 1 < B:
                        where(is_coarse, coarse, b + 1).then_inc(s_coarse, 1)
                    dve.wait_ge(s_coarse, ONE + b + 1)
                    move(nc.vector, b, 0).then_inc(s_numbers, 1)
                dve.wait_ge(s_listed, ONE + B)
                done.step(nc.vector.tensor_copy(summed[:], lists[:, :, :, PARTS, :]))
                for k in reversed(range(1, PARTS)):
                    settle()
                    done.step(nc.vector.tensor_tensor(summed[:], summed[:], lists[:, :, :, k, :], ALU.add))
                settle()
                for i in range(QUARTERS):
                    own = slice(i * FINE, (i + 1) * FINE)
                    for q in range(QUARTERS):
                        part_of = slice(q * FINE, (q + 1) * FINE)
                        rows = slice(i, ROWS, QUARTERS)
                        at = slice(q, COARSE, QUARTERS)
                        done.step(nc.vector.tensor_copy(token[part_of, :, rows],
                                                        lists[own, :, i, 0, at].rearrange("p g c -> p c g")))
                        done.step(nc.vector.tensor_scalar(weight[part_of, :, rows],
                                                          summed[own, :, i, at].rearrange("p g c -> p c g"),
                                                          1.0 / (UP * WS), None, op0=ALU.mult))
                settle()
                done.step(nc.vector.tensor_tensor(flat(idx[:]), flat(token[:]), w["rowbase"][:], ALU.add))
                settle()


def ffn_experts(net, xn_dram, idx, token, weight, out):
    nc, w = net.nc, net.w
    LOOK = 2
    XB = 4
    UNITS = B * E
    with ExitStack() as ctx:
        sb, ps, sem = net.makers(ctx)
        xg = [sb(f"xg{i}", [P, CH, P]) for i in range(XB)]
        xg_hi, xg_lo = ([sb(f"xg_{n}{i}", [P, CAP], F16) for i in range(2)] for n in ("hi", "lo"))
        hid = [sb(f"hid{i}", [P, FC * CAP]) for i in range(2)]
        hid_hi, hid_lo = ([sb(f"hid_{n}{i}", [P, FC, CAP], F16) for i in range(2)] for n in ("hi", "lo"))
        y_hi, y_lo = ([sb(f"y_{n}{i}", [P, CH, P], F16) for i in range(2)] for n in ("hi", "lo"))
        place = [sb(f"place{i}", [P, CH, S], F16) for i in range(2)]
        rounded = sb("rounded", [P, S], BF16)
        psX = ps("psX", [P, 512])
        psH = [ps(f"psH{i}", [P, FC * CAP]) for i in range(2)]
        psY = ps("psY", [P, 512])
        psA = ps("psA", [P, S])
        s_xg = [sem(f"gathered{i}", swdge=True) for i in range(XB)]
        s_xT, s_xhi, s_xlo, s_h, s_gelu = sem("xg_T"), sem("xg_hi"), sem("xg_lo"), sem("h"), sem("gelu")
        s_hhi, s_hlo, s_y, s_yhi, s_ylo = sem("hid_hi"), sem("hid_lo"), sem("y"), sem("y_hi"), sem("y_lo")
        s_place, s_back, s_round, s_added, s_out = sem("place"), sem("rows_back"), sem("rounded"), sem("added"), sem("stored")

        def parts(hi, lo):
            return ((hi[0], hi[1]), (hi[0], lo[1]), (lo[0], hi[1]))

        net.raise_sems()
        with nc.Block() as block:
            @block.gpsimd
            def _(pool):
                for n in range(UNITS + LOOK + 1):
                    if n >= XB:
                        pool.wait_ge(s_xT, ONE + n - XB + 1)
                    r = n % UNITS
                    for c in range(CH):
                        pool.indirect_dma_start(xg[n % XB][:, c, :], None, xn_dram,
                                                bass.IndirectOffsetOnAxis(ap=idx[:, c, r:r + 1], axis=0)
                                                ).then_inc(s_xg[n % XB], 16)

            @block.tensor
            def _(pe):
                def turn(b, u):
                    pe.wait_ge(s_xg[u % XB], 16 * CH * (b * (E // XB) + u // XB + 1))
                    pe.wait_ge(s_xlo, ONE + b * E + u)
                    for c in range(CH):
                        last = pe.transpose(psX[:, c * P:(c + 1) * P], xg[u % XB][:, c, :], w["ident"][:])
                    last.then_inc(s_xT, 1)

                def up(b, u):
                    pe.wait_ge(s_xlo, ONE + b * E + u + 1)
                    pe.wait_ge(s_gelu, ONE + b * E + u - 1)
                    for f in range(FC):
                        col = (u % E * FC + f) * P
                        for i, (l, r) in enumerate(((net.hi, xg_hi), (net.hi, xg_lo), (net.lo, xg_hi))):
                            last = pe.matmul(psH[u % 2][:, f * CAP:(f + 1) * CAP], l["w1"][:, col:col + P], r[u % 2][:],
                                             start=(i == 0), stop=(i == 2))
                    last.then_inc(s_h, 1)

                def down(b, u):
                    pe.wait_ge(s_hlo, ONE + b * E + u + 1)
                    pe.wait_ge(s_ylo, ONE + b * E + u)
                    for c in range(CH):
                        for f in range(FC):
                            col = (u % E * FC + f) * P
                            for i, (l, r) in enumerate(((hid_hi, net.hi), (hid_hi, net.lo), (hid_lo, net.hi))):
                                last = pe.matmul(psY[:, c * P:(c + 1) * P], l[u % 2][:, f, c * P:(c + 1) * P],
                                                 r["w2"][:, col:col + P], start=(f == 0 and i == 0),
                                                 stop=(f == FC - 1 and i == 2))
                    last.then_inc(s_y, 1)

                def back(b, u):
                    pe.wait_ge(s_ylo, ONE + b * E + u + 1)
                    pe.wait_ge(s_place, ONE + b * E + u + 1)
                    if u == 0:
                        pe.wait_ge(s_round, ONE + b)
                    for t in range(T):
                        for c in range(CH):
                            for i, r in enumerate((y_hi, y_lo)):
                                last = pe.matmul(psA[:, t * P:(t + 1) * P], place[u % 2][:, c, t * P:(t + 1) * P],
                                                 r[u % 2][:, c, :], start=(u == 0 and t % 4 == 0 and c == 0 and i == 0),
                                                 stop=(u == E - 1 and c == CH - 1 and i == 1), skip_group_check=True)
                    last.then_inc(s_back, 1)

                turn(0, 0)
                for u in range(LOOK):
                    up(0, u)
                    turn(0, u + 1)
                with pe.Fori(0, B) as b:
                    for u in range(E):
                        down(b, u)
                        up(b, u + LOOK)
                        turn(b, u + LOOK + 1)
                        back(b, u)

            @block.scalar
            def _(act):
                def cast(b, u):
                    act.wait_ge(s_xT, ONE + b * E + u + 1)
                    act.wait_ge(s_h, ONE + b * E + u - 1)
                    nc.scalar.activation(xg_hi[u % 2][:], psX[:, 0:CAP], ACT.Copy).then_inc(s_xhi, 1)

                def gelu(b, u):
                    act.wait_ge(s_h, ONE + b * E + u + 1)
                    act.wait_ge(s_hlo, ONE + b * E + u - 1)
                    nc.scalar.activation(hid[u % 2][:], psH[u % 2][:], ACT.Gelu_apprx_tanh,
                                         scale=1.0 / WS).then_inc(s_gelu, 1)

                def weigh(b, u):
                    act.wait_ge(s_y, ONE + b * E + u + 1)
                    act.wait_ge(s_back, ONE + b * E + u - 1)
                    for c in range(CH):
                        nc.scalar.activation(y_hi[u % 2][:, c, :], psY[:, c * P:(c + 1) * P], ACT.Copy,
                                             scale=weight[:, c, bass.ds(b * E + u, 1)]).then_inc(s_yhi, 1)

                cast(0, 0)
                for u in range(LOOK):
                    gelu(0, u)
                    cast(0, u + 1)
                with act.Fori(0, B) as b:
                    for u in range(E):
                        weigh(b, u)
                        gelu(b, u + LOOK)
                        cast(b, u + LOOK + 1)

            @block.vector
            def _(dve):
                def low(b, u):
                    dve.wait_ge(s_xhi, ONE + b * E + u + 1)
                    nc.vector.tensor_tensor(xg_lo[u % 2][:], psX[:, 0:CAP], xg_hi[u % 2][:], ALU.subtract).then_inc(s_xlo, 1)

                def split(b, u):
                    dve.wait_ge(s_gelu, ONE + b * E + u + 1)
                    dve.wait_ge(s_y, ONE + b * E + u - 1)
                    nc.vector.tensor_copy(hid_hi[u % 2][:].rearrange("p f s -> p (f s)"), hid[u % 2][:]).then_inc(s_hhi, 1)
                    dve.wait_ge(s_hhi, ONE + b * E + u + 1)
                    nc.vector.tensor_tensor(hid_lo[u % 2][:].rearrange("p f s -> p (f s)"), hid[u % 2][:],
                                            hid_hi[u % 2][:].rearrange("p f s -> p (f s)"), ALU.subtract).then_inc(s_hlo, 1)

                def places(b, u):
                    dve.wait_ge(s_back, ONE + b * E + u - 1)
                    for c in range(CH):
                        last = nc.vector.tensor_scalar(place[u % 2][:, c, :], w["iota"][:], token[:, c, bass.ds(b * E + u, 1)],
                                                       None, op0=ALU.is_equal)
                    last.then_inc(s_place, 1)

                def weigh_low(b, u):
                    dve.wait_ge(s_yhi, ONE + CH * (b * E + u + 1))
                    for c in range(CH):
                        last = nc.vector.scalar_tensor_tensor(y_lo[u % 2][:, c, :], psY[:, c * P:(c + 1) * P],
                                                              weight[:, c, bass.ds(b * E + u, 1)], y_hi[u % 2][:, c, :],
                                                              ALU.mult, ALU.subtract)
                    last.then_inc(s_ylo, 1)

                low(0, 0)
                for u in range(LOOK):
                    split(0, u)
                    low(0, u + 1)

                def finish(b):
                    dve.wait_ge(s_round, ONE + b + 1)
                    rows = net.x[:, bass.ds(b * T, T), :]
                    nc.vector.tensor_tensor(rows, rows, rounded[:].rearrange("p (t c) -> p t c", t=T),
                                            ALU.add).then_inc(s_added, 1)
                    if out is None:
                        dve.wait_ge(s_added, ONE + b + 1)
                        tile_stats(net, b, range(T))

                def sequence(b, before):
                    for u in range(E):
                        places(b, u)
                        weigh_low(b, u)
                        split(b, u + LOOK)
                        low(b, u + LOOK + 1)
                        if before is not None and u == 2:
                            finish(before)
                    dve.wait_ge(s_back, ONE + b * E + E)
                    if before is not None:
                        dve.wait_ge(s_added, ONE + b)
                    nc.vector.tensor_copy(rounded[:], psA[:]).then_inc(s_round, 1)

                sequence(0, None)
                with dve.Fori(0, B - 1) as b:
                    sequence(b + 1, b)
                finish(B - 1)

            @block.sync
            def _(sp):
                if out is not None:
                    out_tiles = out.rearrange("(t p) c -> p t c", p=P)
                    for b in range(B):
                        sp.wait_ge(s_added, ONE + b + 1)
                        sp.dma_start(out_tiles[:, b * T:(b + 1) * T, :], net.x[:, b * T:(b + 1) * T, :]).then_inc(s_out, 16)
                    sp.wait_ge(s_out, ONE + 16 * B)


def attention_b(net):
    nc, w = net.nc, net.w
    PAIRS = GROUP * T // 2
    PROJ = GROUP + 2
    HEAD = [("pair", 0), ("pair", 1), ("proj", 0), ("pair", 2), ("pair", 3), ("proj", 1),
            ("pair", 4), ("pair", 5), ("proj", 2), ("pair", 6), ("pair", 7), ("proj", 3)]
    STEPS, LOOK = NKV * len(HEAD), 2
    NP = NKV * PAIRS
    SLOTS = {k - PROJ: ("proj", k) for k in range(PROJ)}
    for k in range(STEPS + LOOK):
        kind, i = HEAD[k % len(HEAD)]
        j = k // len(HEAD)
        SLOTS[k] = (kind, j * PAIRS + i if kind == "pair" else (j + 1) * PROJ + i)
    HALF = P // 2
    CHUNKS = 3
    with ExitStack() as ctx:
        sb, ps, sem = net.makers(ctx)
        work = sb("work", [P, 4, NT])
        mean, rstd = sb("mean", [P, NT]), sb("rstd", [P, NT])
        xT_hi, xT_lo = sb("xT_hi", [P, (B + 1) * S], F16), sb("xT_lo", [P, (B + 1) * S], F16)
        qk_hi = [[sb(f"qk_hi{r}{i}", [P, S], F16) for i in range(GROUP + 1)] for r in range(2)]
        qk_lo = [[sb(f"qk_lo{r}{i}", [P, S], F16) for i in range(GROUP + 1)] for r in range(2)]
        v = [sb(f"v{r}", [P, S]) for r in range(2)]
        by_cos, by_sin = [sb(f"by_cos{i}", [P, S]) for i in range(2)], [sb(f"by_sin{i}", [P, S]) for i in range(2)]
        prob = [[sb(f"prob{z}{r}", [P, S // (1 + z)]) for r in range(2)] for z in range(2)]
        probT = [[sb(f"probT{z}{r}", [P, S // (1 + z)]) for r in range(2)] for z in range(2)]
        nmax, nbias, rowsum, rinv = (sb(n, [P, 2, NP]) for n in ("nmax", "nbias", "rowsum", "rinv"))
        oT = sb("oT", [P, NH, T, P])
        psS = [ps(f"psS{i}", [P, S]) for i in range(2)]
        psM = ps("psM", [P, 512])
        psT = ps("psT", [P, S])
        psO = ps("psO", [P, 512])
        s_var, s_std, s_dve = sem("var"), sem("std"), sem("dve")
        s_xs, s_xT, s_xhi, s_xlo = sem("xs"), sem("xT"), sem("x_hi"), sem("x_lo")
        s_slot = sem("slot_written")
        s_rope, s_rot, s_rsum, s_v = sem("roped"), sem("rotated"), sem("rot_sum"), sem("v")
        s_s, s_nb, s_exp, s_p = ([sem(f"{n}{z}") for z in range(2)] for n in ("scores", "nbias", "exp", "p"))
        s_T, s_Ts, s_o, s_os, s_y, s_ys = sem("p_T"), sem("pT_sb"), sem("o"), sem("oT_sb"), sem("y"), sem("y_added")

        def unit(a, z):
            m = a % (T // 2)
            return a % PAIRS // (T // 2), (T - 1 - m if z == 0 else m), a // PAIRS

        def score_bank(k, z):
            return psM if z else psS[k % 2]

        def slot_of(a):
            return a // PAIRS * len(HEAD) + (0, 1, 3, 4, 6, 7, 9, 10)[a % PAIRS]

        def until(eng, s, b, per, n):
            if isinstance(b, int) and b * per + n <= 0:
                return
            eng.wait_ge(s, ONE + b * per + n)

        def pe_scores(pe, b, a, z):
            g, q, j = unit(a, z)
            r, width, k = j % 2, (q + 1) * P, slot_of(a)
            bank, rows = score_bank(k, z), slice(q * P, (q + 1) * P)
            if z:
                until(pe, s_exp[1], b, NP, a)
            if a % (T // 2) == 0:
                until(pe, s_rot, b, NKV * (GROUP + 1), j * (GROUP + 1) + 2 + g)
            for c in range(0, width, 512):
                end = min(width, c + 512)
                for i, (l, rr) in enumerate(((qk_hi, qk_hi), (qk_hi, qk_lo), (qk_lo, qk_hi))):
                    last = pe.matmul(bank[:, c:end], l[r][1 + g][:, rows], rr[r][0][:, c:end],
                                     start=(i == 0), stop=(i == 2 and end < width))
            last = pe.matmul(bank[:, q * P:width], w["identb"][:], w["maskb"][:], start=False, stop=True)
            last.then_inc(s_s[z], 1)

        def pe_proj(pe, b, k, n):
            j, i = divmod(n, PROJ)
            parts = (("hi", xT_hi), ("hi", xT_lo), ("lo", xT_hi))
            seq, j = (b + 1, 0) if j == NKV else (b, j)
            bank = psS[k % 2]
            if i < GROUP + 1:
                key, col = ("wk", j * P) if i == 0 else ("wq", (j * GROUP + i - 1) * P)
                for c in range(2):
                    cols = bass.ds(seq * S + c * 512, 512)
                    for m, (part, src) in enumerate(parts):
                        wt = (net.hi if part == "hi" else net.lo)[key]
                        last = pe.matmul(bank[:, c * 512:(c + 1) * 512], wt[:, col:col + P], src[:, cols],
                                         start=(m == 0), stop=(m == 2))
            else:
                for t in range(T):
                    for m, (part, src) in enumerate(parts):
                        wt = (net.hi if part == "hi" else net.lo)["wv"]
                        last = pe.matmul(bank[:, t * P:(t + 1) * P], src[:, bass.ds(seq * S + t * P, P)],
                                         wt[:, j * P:(j + 1) * P], start=(m == 0), stop=(m == 2))
            last.then_inc(s_slot, 1)

        def pe_write(pe, b, k):
            kind, n = SLOTS[k]
            if k - 2 >= -PROJ:
                before, m = SLOTS[k - 2]
                if before == "pair":
                    until(pe, s_exp[0], b, NP, m + 1)
                elif m % PROJ < GROUP + 1:
                    until(pe, s_rope, b, 3 * NKV * (GROUP + 1), 3 * (m // PROJ * (GROUP + 1) + m % PROJ + 1))
                else:
                    until(pe, s_v, b, NKV, m // PROJ + 1)
            if kind == "pair":
                pe_scores(pe, b, n, 0)
            else:
                pe_proj(pe, b, k, n)

        def pe_turn(pe, b, a, z):
            g, q, j = unit(a, z)
            until(pe, s_p[z], b, NP, a + 1)
            for c in range(0, q + 1, 4):
                n = CHUNKS * a + (2 if z else c // 4)
                until(pe, s_Ts, b, CHUNKS * NP, n - 1)
                for i in range(c, min(q + 1, c + 4)):
                    at = n % 2 * 512 + (i - c) * P
                    last = pe.transpose(psT[:, at:at + P], prob[z][a % 2][:, i * P:(i + 1) * P], w["ident"][:])
                last.then_inc(s_T, 1)

        def pe_values(pe, b, a, z):
            g, q, j = unit(a, z)
            until(pe, s_Ts, b, CHUNKS * NP, CHUNKS * a + (3 if z else 2))
            if not z:
                until(pe, s_os, b, NP, a)
                if a % PAIRS == 0:
                    until(pe, s_v, b, NKV, j + 1)
            for i in range(q + 1):
                last = pe.matmul(psO[:, (1 - z) * P:(2 - z) * P], v[j % 2][:, i * P:(i + 1) * P],
                                 probT[z][a % 2][:, i * P:(i + 1) * P], start=(i == 0), stop=(i == q))
            last.then_inc(s_o, 1)

        def xs_of(b):
            return prob[0][b % 2]

        def dve_xT_low(dve, b):
            dve.wait_ge(s_xhi, ONE + b + 1)
            nc.vector.tensor_tensor(xT_lo[:, b * S:(b + 1) * S], psT[:], xT_hi[:, b * S:(b + 1) * S],
                                    ALU.subtract).then_inc(s_xlo, 1)

        def dve_rope(dve, b, k, n):
            j, i = divmod(n, PROJ)
            m = j * (GROUP + 1) + i
            until(dve, s_slot, b, NKV * PROJ, n + 1)
            until(dve, s_rot, b, NKV * (GROUP + 1), m - 1)
            src = psS[k % 2]
            nc.vector.tensor_tensor(by_cos[m % 2][:], src[:], w["cos"][:], ALU.mult).then_inc(s_rope, 1)
            for lo, hi in ((0, HALF), (HALF, 0)):
                nc.vector.tensor_tensor(by_sin[m % 2][lo:lo + HALF, :], src[hi:hi + HALF, :], w["sin"][hi:hi + HALF, :],
                                        ALU.mult).then_inc(s_rope, 1)

        def dve_max(dve, b, a, z, done):
            g, q, j = unit(a, z)
            until(dve, s_s[z], b, NP, a + 1)
            done.step(nc.vector.reduce_max(nmax[:, z, a % NP:a % NP + 1], score_bank(slot_of(a), z)[:, 0:(q + 1) * P], AX_X,
                                           negate=True))
            dve.wait_ge(done.sem, done.at)
            nc.vector.tensor_scalar(nbias[:, z, a % NP:a % NP + 1], nmax[:, z, a % NP:a % NP + 1], SCALE / (WS * WS), None,
                                    op0=ALU.mult).then_inc(s_nb[z], 1)

        def dve_divide(dve, b, a, z, done):
            g, q, j = unit(a, z)
            until(dve, s_exp[z], b, NP, a + 1)
            done.step(nc.vector.reciprocal(rinv[:, z, a % NP:a % NP + 1], rowsum[:, z, a % NP:a % NP + 1]))
            dve.wait_ge(done.sem, done.at)
            p = prob[z][a % 2][:, 0:(q + 1) * P]
            nc.vector.tensor_scalar(p, p, rinv[:, z, a % NP:a % NP + 1], 1.0 / WS, op0=ALU.mult, op1=ALU.mult).then_inc(s_p[z], 1)

        def dve_take(dve, b, k, done):
            kind, n = SLOTS[k]
            if kind == "pair":
                dve_max(dve, b, n, 0, done)
            elif n % PROJ < GROUP + 1:
                dve_rope(dve, b, k, n)

        def act_exp(act, b, a, z):
            g, q, j = unit(a, z)
            until(act, s_nb[z], b, NP, a + 1)
            until(act, s_T, b, CHUNKS * NP, CHUNKS * (a - 2) + (3 if z else 2))
            width = (q + 1) * P
            nc.scalar.activation(prob[z][a % 2][:, 0:width], score_bank(slot_of(a), z)[:, 0:width], ACT.Exp,
                                 bias=nbias[:, z, a % NP:a % NP + 1], scale=SCALE / (WS * WS),
                                 accum_out=rowsum[:, z, a % NP:a % NP + 1]).then_inc(s_exp[z], 1)

        def act_take(act, b, k):
            kind, n = SLOTS[k]
            if kind == "pair":
                act_exp(act, b, n, 0)
            elif n % PROJ == GROUP + 1:
                until(act, s_slot, b, NKV * PROJ, n + 1)
                j = n // PROJ
                until(act, s_o, b, 2 * NP, 2 * PAIRS * (j - 1))
                nc.scalar.activation(v[j % 2][:], psS[k % 2][:], ACT.Copy).then_inc(s_v, 1)

        def act_probT(act, b, a, z):
            g, q, j = unit(a, z)
            for c in range(0, q + 1, 4):
                n = CHUNKS * a + (2 if z else c // 4)
                until(act, s_T, b, CHUNKS * NP, n + 1)
                width = (min(q + 1, c + 4) - c) * P
                until(act, s_o, b, 2 * NP, 2 * (a - 2) + 1 + z)
                nc.scalar.activation(probT[z][a % 2][:, c * P:c * P + width], psT[:, n % 2 * 512:n % 2 * 512 + width],
                                     ACT.Copy).then_inc(s_Ts, 1)

        def act_oT(act, b, a):
            g, q, j = unit(a, 1)
            until(act, s_o, b, 2 * NP, 2 * a + 2)
            if a == 0:
                until(act, s_y, b, 2, 0)
            out = oT[:, j * GROUP + g, q:T - q:T - 1 - 2 * q, :]
            nc.scalar.activation(out, psO[:, 0:2 * P].rearrange("p (z c) -> p z c", z=2), ACT.Copy).then_inc(s_os, 1)

        net.raise_sems()
        with nc.Block() as block:
            @block.tensor
            def _(pe):
                for k in range(-PROJ, LOOK):
                    b = k + PROJ
                    if b < B:
                        pe.wait_ge(s_xs, ONE + (b + 1) * T)
                        if b:
                            pe.wait_ge(s_xlo, ONE + b + 1)
                        for t in range(T):
                            last = pe.transpose(psT[:, t * P:(t + 1) * P], xs_of(b)[:, t * P:(t + 1) * P], w["ident"][:])
                        last.then_inc(s_xT, 1)
                    if b == 0:
                        pe.wait_ge(s_xlo, ONE + 2)
                    pe_write(pe, 0, k)
                pe_scores(pe, 0, 0, 1)
                with pe.Fori(0, B) as b:
                    for k in range(STEPS):
                        kind, a = SLOTS[k]
                        if kind == "pair":
                            if a == 0:
                                until(pe, s_ys, b, 2, 0)
                            pe_turn(pe, b, a, 0)
                            pe_scores(pe, b, a + 1, 1)
                        pe_write(pe, b, k + LOOK)
                        if kind == "pair":
                            pe_turn(pe, b, a, 1)
                            pe_values(pe, b, a, 0)
                            pe_values(pe, b, a, 1)
                    until(pe, s_os, b, NP, NP)
                    until(pe, s_Ts, b, CHUNKS * NP, CHUNKS * NP)
                    for t in range(T):
                        for h in range(NH):
                            last = pe.matmul(psT[:, t * P:(t + 1) * P], oT[:, h, t, :], w["wo"][:, h * P:(h + 1) * P],
                                             start=(h == 0), stop=(h == NH - 1))
                        if t % 4 == 3:
                            last.then_inc(s_y, 1)

            @block.vector
            def _(dve):
                done, var, std = Steps(s_dve), Steps(s_var), Steps(s_std)
                nc.vector.memset(xT_hi[:, B * S:], 0.0).then_inc(s_xlo, 1)
                nc.vector.memset(xT_lo[:, B * S:], 0.0).then_inc(s_dve, 1)
                done.expect()
                norm_stats(nc, dve, done, var, std, net.stats, work, mean[:], rstd[:])

                def norm_x(b):
                    if b >= 2:
                        dve.wait_ge(s_xT, ONE + b - 1)
                    for t in range(T):
                        i = b * T + t
                        nc.vector.tensor_scalar(xs_of(b)[:, t * P:(t + 1) * P], net.x[:, i, :], mean[:, i:i + 1],
                                                rstd[:, i:i + 1], op0=ALU.subtract, op1=ALU.mult).then_inc(s_xs, 1)

                norm_x(0)
                norm_x(1)
                for k in range(-PROJ, LOOK):
                    b = k + PROJ
                    if b < B:
                        dve_xT_low(dve, b)
                        if b + 2 < B:
                            norm_x(b + 2)
                    dve_take(dve, 0, k, done)
                dve_max(dve, 0, 0, 1, done)
                dve_divide(dve, 0, 0, 0, done)
                with dve.Fori(0, B) as b:
                    done.enter(b, 4 * NP)
                    for k in range(STEPS):
                        kind, a = SLOTS[k]
                        if kind == "pair":
                            dve_divide(dve, b, a, 1, done)
                        if SLOTS[k + 1][0] == "pair":
                            dve_divide(dve, b, SLOTS[k + 1][1], 0, done)
                        if kind == "pair":
                            dve_max(dve, b, a + 1, 1, done)
                        dve_take(dve, b, k + LOOK, done)
                    done.leave(B)
                    for c in range(2):
                        until(dve, s_y, b, 2, c + 1)
                        rows = net.x[:, bass.ds(b * T + c * 4, 4), :]
                        nc.vector.tensor_tensor(rows, psT[:, c * 512:(c + 1) * 512].rearrange("p (t c) -> p t c", t=4), rows,
                                                ALU.add).then_inc(s_ys, 1)
                        dve.wait_ge(s_ys, ONE + 2 * b + c + 1)
                        tile_stats(net, b, range(c * 4, (c + 1) * 4))

            @block.gpsimd
            def _(pool):
                R = GROUP + 1

                def rotate(n, i, r):
                    m = (r * R + i) % 2
                    cos, sin, hi, lo = by_cos[m], by_sin[m], qk_hi[r][i], qk_lo[r][i]
                    if i == 0 and not isinstance(n, int):
                        pool.wait_ge(s_s[0], ONE + n * PAIRS - PAIRS)
                        pool.wait_ge(s_s[1], ONE + n * PAIRS - PAIRS)
                    pool.wait_ge(s_rope, ONE + 3 * (n * R + i + 1))
                    nc.gpsimd.tensor_tensor(hi[:], cos[:], sin[:], ALU.add).then_inc(s_rsum, 1)
                    nc.gpsimd.tensor_tensor(cos[:], cos[:], sin[:], ALU.add).then_inc(s_rsum, 1)
                    pool.wait_ge(s_rsum, ONE + 2 * (n * R + i + 1))
                    nc.gpsimd.tensor_tensor(lo[:], cos[:], hi[:], ALU.subtract).then_inc(s_rot, 1)

                for i in range(R):
                    rotate(0, i, 0)
                with pool.Fori(0, B * NKV // 2) as h:
                    for r in range(2):
                        for i in range(R):
                            rotate(2 * h + r + 1, i, 1 - r)

            @block.scalar
            def _(act):
                act.wait_ge(s_var, ONE + 1)
                nc.scalar.activation(work[:, 2, :], work[:, 2, :], ACT.Sqrt).then_inc(s_std, 1)
                for b in range(B):
                    act.wait_ge(s_xT, ONE + b + 1)
                    nc.scalar.activation(xT_hi[:, b * S:(b + 1) * S], psT[:], ACT.Copy).then_inc(s_xhi, 1)
                for k in range(-PROJ, LOOK):
                    act_take(act, 0, k)
                act_exp(act, 0, 0, 1)
                with act.Fori(0, B) as b:
                    for k in range(STEPS):
                        kind, a = SLOTS[k]
                        if kind == "pair":
                            act_probT(act, b, a, 0)
                            act_exp(act, b, a + 1, 1)
                            act_probT(act, b, a, 1)
                        act_take(act, b, k + LOOK)
                        if kind == "pair":
                            act_oT(act, b, a)


def build(nc, d, out):
    with ExitStack() as ctx:
        net = Net(nc, ctx)
        with ExitStack() as first:
            load_stage(net, d, first)
            attention_a(net)
        xn_dram = nc.dram_tensor("xn", (B * S, P), F32, kind="Internal").ap()
        ffn(net, xn_dram)
        attention_b(net)
        ffn(net, xn_dram, out)


def kernel(**inputs):
    import ml_dtypes
    import numpy as np
    import concourse.bacc as bacc
    from concourse.bass_utils import run_bass_kernel_spmd

    a = {k: np.asarray(v) for k, v in inputs.items()}
    lay = np.ascontiguousarray
    wqkv = a["L0_attn_a_w_qkv"]
    arrays = {
        "x": lay(a["L0_attn_a_x"].reshape(B * S, P)),
        "wq_a": lay(wqkv[0:P]), "wk_a": lay(wqkv[P:2 * P]), "wv_aT": lay(wqkv[2 * P:].T),
        "wfc_T": lay(a["L0_attn_a_w_fc"].T),
        "bfc": lay(np.broadcast_to(a["L0_attn_a_b_fc"], (P, P))),
        "gamma": lay(np.broadcast_to(a["L0_attn_a_gamma"], (P, P))),
        "beta": lay(np.broadcast_to(a["L0_attn_a_beta"], (P, P))),
        "gate": a["L0_ffn_gate_w"],
        "wq": a["L0_attn_b_Wq"], "wk": a["L0_attn_b_Wk"], "wv": a["L0_attn_b_Wv"],
        "wo": lay(a["L0_attn_b_Wo"].reshape(NH, P, P).transpose(1, 0, 2).reshape(P, NH * P)),
        "w1": lay(a["L0_ffn_w1"].transpose(1, 0, 2).reshape(P, E * FC * P)),
        "w2": lay(a["L0_ffn_w2"].reshape(E, FC, P, P).transpose(2, 0, 1, 3).reshape(P, E * FC * P)),
    }
    half = np.arange(0, P, 2, dtype=np.float32) / np.float32(P)
    inv_freq = (np.float32(1.0) / np.power(np.float32(10000.0), half)).astype(np.float32)
    angle = np.outer(inv_freq, np.arange(S, dtype=np.float32)).astype(np.float32)
    arrays["cos"] = lay(np.concatenate([np.cos(angle)] * 2).astype(np.float32))
    arrays["sin"] = lay(np.concatenate([np.sin(angle), -np.sin(angle)]).astype(np.float32))
    arrays["ident"] = np.eye(P, dtype=np.float32)
    arrays["identb"] = np.eye(P, dtype=ml_dtypes.bfloat16)
    arrays["maskb"] = np.triu(np.full((P, P), -1e30, np.float32), 1).astype(ml_dtypes.bfloat16)
    arrays["iota"] = lay(np.broadcast_to(np.arange(S), (P, S)).astype(np.float16))
    arrays["rowbase"] = lay(np.broadcast_to(np.arange(CH * ROWS) % ROWS // E * S, (P, CH * ROWS)).astype(np.float32))
    arrays["number"] = lay(np.arange(S, dtype=np.float32).reshape(T, P).T)
    arrays["ones"] = np.ones((P, P), np.float16)
    arrays["upto"] = np.triu(np.ones((P, P), np.float16))
    nc = bacc.Bacc("TRN2", target_bir_lowering=False, num_devices=1)
    d = {k: nc.dram_tensor(f"in_{k}", v.shape, mybir.dt.from_np(v.dtype), kind="ExternalInput").ap()
         for k, v in arrays.items()}
    out = nc.dram_tensor("out", (B * S, P), F32, kind="ExternalOutput").ap()
    build(nc, d, out)
    r = run_bass_kernel_spmd(nc, [{f"in_{k}": v for k, v in arrays.items()}], core_ids=[0])
    return r.results[0]["out"].reshape(B, S, P)
```
